# Optimizing a Trainium2 kernel written in Bass

```python
import numpy as np
import jax
import jax.numpy as jnp

def _softmax(x, axis=-1):
    return jax.nn.softmax(x, axis=axis)

def _gelu(x):
    return jax.nn.gelu(x, approximate=True)

def _silu(x):
    return jax.nn.silu(x)

def _sigmoid(x):
    return jax.nn.sigmoid(x)

def _layernorm(x, axis=-1, eps=1e-05):
    m = jnp.mean(x, axis=axis, keepdims=True)
    v = jnp.var(x, axis=axis, keepdims=True)
    return (x - m) / jnp.sqrt(v + eps)

def _scatter_add(tgt, idx, src, axis=0):
    return tgt.at[idx].add(src)

def _segment_sum(src, seg, n):
    return jax.ops.segment_sum(src, seg, n)
kernel_name = 'mk_macaron_d1_jaxref_r8_0ca6c4'

def setup_inputs(seed: int=0):
    np.random.seed(seed)
    _w = jnp.asarray

    def _L0_attn_setup():
        import jax, jax.numpy as jnp
        import numpy as np
        B, S, H = (8, 512, 128)
        WIN = 128
        TOPK = max(1, int(WIN * 0.25))
        EPS = 1e-05
        NEG_SLOPE = 0.01
        key = jax.random.key(seed)
        ks = jax.random.split(key, 8)
        w_scale = 1.0 / np.sqrt(H)
        return {'x': jax.random.normal(ks[0], (B, S, H), jnp.float32), 'Wq': jax.random.uniform(ks[1], (H, H), jnp.float32, -w_scale, w_scale), 'bq': jax.random.uniform(ks[2], (H,), jnp.float32, -w_scale, w_scale), 'Wk': jax.random.uniform(ks[3], (H, H), jnp.float32, -w_scale, w_scale), 'bk': jax.random.uniform(ks[4], (H,), jnp.float32, -w_scale, w_scale), 'Wv': jax.random.uniform(ks[5], (H, H), jnp.float32, -w_scale, w_scale), 'bv': jax.random.uniform(ks[6], (H,), jnp.float32, -w_scale, w_scale), 'gamma': jnp.ones((H,), jnp.float32), 'beta': jnp.zeros((H,), jnp.float32)}
    _L0_attn_in = _L0_attn_setup()

    def _L0_ffn_setup():
        import jax, jax.numpy as jnp
        import numpy as np
        LN_EPS = 1e-05

        def _swiglu(h, w_gate_up, w_down):
            gu = h @ w_gate_up.T
            gate, up = jnp.split(gu, 2, axis=-1)
            return jax.nn.silu(gate) * up @ w_down.T
        key = jax.random.key(seed)
        ks = jax.random.split(key, 6)
        d_model, d_ff, E = (128, 512, 8)
        shared_d_ff = d_ff // 4
        routed_d_ff = d_ff - shared_d_ff
        B, S = (4, 256)
        x = jax.random.normal(ks[0], (B, S, d_model), dtype=jnp.float32)
        ln_gamma = jnp.ones((d_model,), jnp.float32)
        ln_beta = jnp.zeros((d_model,), jnp.float32)
        router_w = jax.random.normal(ks[1], (E, d_model), jnp.float32) * 0.02
        gate_up_w = jax.random.normal(ks[2], (E, 2 * routed_d_ff, d_model), jnp.float32) * (1.0 / np.sqrt(d_model))
        down_w = jax.random.normal(ks[3], (E, d_model, routed_d_ff), jnp.float32) * (1.0 / np.sqrt(routed_d_ff))
        shared_gate_up_w = jax.random.normal(ks[4], (2 * shared_d_ff, d_model), jnp.float32) * (1.0 / np.sqrt(d_model))
        shared_down_w = jax.random.normal(ks[5], (d_model, shared_d_ff), jnp.float32) * (1.0 / np.sqrt(shared_d_ff))
        return dict(x=x, ln_gamma=ln_gamma, ln_beta=ln_beta, router_w=router_w, gate_up_w=gate_up_w, down_w=down_w, shared_gate_up_w=shared_gate_up_w, shared_down_w=shared_down_w)
    _L0_ffn_in = _L0_ffn_setup()
    _d = {'L0_attn_x': _L0_attn_in['x'], 'L0_attn_Wq': _L0_attn_in['Wq'], 'L0_attn_bq': _L0_attn_in['bq'], 'L0_attn_Wk': _L0_attn_in['Wk'], 'L0_attn_bk': _L0_attn_in['bk'], 'L0_attn_Wv': _L0_attn_in['Wv'], 'L0_attn_bv': _L0_attn_in['bv'], 'L0_attn_gamma': _L0_attn_in['gamma'], 'L0_attn_beta': _L0_attn_in['beta'], 'L0_ffn_ln_gamma': _L0_ffn_in['ln_gamma'], 'L0_ffn_ln_beta': _L0_ffn_in['ln_beta'], 'L0_ffn_router_w': _L0_ffn_in['router_w'], 'L0_ffn_gate_up_w': _L0_ffn_in['gate_up_w'], 'L0_ffn_down_w': _L0_ffn_in['down_w'], 'L0_ffn_shared_gate_up_w': _L0_ffn_in['shared_gate_up_w'], 'L0_ffn_shared_down_w': _L0_ffn_in['shared_down_w']}
    _x0 = _d['L0_attn_x']
    _d['L0_attn_x'] = jax.random.normal(jax.random.fold_in(jax.random.key(seed), 1), (8, 512, 128), dtype=_x0.dtype)
    del _x0
    return _d

def reference(L0_attn_x, L0_attn_Wq, L0_attn_bq, L0_attn_Wk, L0_attn_bk, L0_attn_Wv, L0_attn_bv, L0_attn_gamma, L0_attn_beta, L0_ffn_ln_gamma, L0_ffn_ln_beta, L0_ffn_router_w, L0_ffn_gate_up_w, L0_ffn_down_w, L0_ffn_shared_gate_up_w, L0_ffn_shared_down_w):

    def _L0_attn_ref(x, Wq, bq, Wk, bk, Wv, bv, gamma, beta):
        import jax, jax.numpy as jnp
        import numpy as np
        B, S, H = (8, 512, 128)
        WIN = 128
        TOPK = max(1, int(WIN * 0.25))
        EPS = 1e-05
        NEG_SLOPE = 0.01
        b, s, h = x.shape
        nw = s // WIN
        xw = x.reshape(b, nw, WIN, h)
        q = jnp.einsum('bnwh,oh->bnwo', xw, Wq) + bq
        k = jnp.einsum('bnwh,oh->bnwo', xw, Wk) + bk
        v = jnp.einsum('bnwh,oh->bnwo', xw, Wv) + bv
        scores = jnp.einsum('bnqh,bnkh->bnqk', q, k) / np.float32(np.sqrt(H))
        _, top_idx = jax.lax.top_k(scores, TOPK)
        mask = jnp.put_along_axis(jnp.zeros(scores.shape, bool), top_idx, True, axis=-1, inplace=False)
        masked = jnp.where(mask, scores, -jnp.inf)
        masked = masked - jnp.max(masked, axis=-1, keepdims=True)
        attn = jax.nn.softmax(masked, axis=-1)
        out = jnp.einsum('bnqk,bnkh->bnqh', attn, v).reshape(b, s, h)
        out = jnp.where(out >= 0, out, NEG_SLOPE * out)
        r = out + x
        mu = jnp.mean(r, axis=-1, keepdims=True)
        var = jnp.var(r, axis=-1, keepdims=True)
        return (r - mu) / jnp.sqrt(var + EPS) * gamma + beta

    def _L0_ffn_ref(x, ln_gamma, ln_beta, router_w, gate_up_w, down_w, shared_gate_up_w, shared_down_w):
        import jax, jax.numpy as jnp
        import numpy as np
        LN_EPS = 1e-05

        def _swiglu(h, w_gate_up, w_down):
            gu = h @ w_gate_up.T
            gate, up = jnp.split(gu, 2, axis=-1)
            return jax.nn.silu(gate) * up @ w_down.T
        B, S, D = x.shape
        E = router_w.shape[0]
        top_k = 2
        xt = x.reshape(-1, D)
        mu = jnp.mean(xt, axis=-1, keepdims=True)
        var = jnp.mean(jnp.square(xt - mu), axis=-1, keepdims=True)
        normed = (xt - mu) * jax.lax.rsqrt(var + LN_EPS) * ln_gamma + ln_beta
        logits = normed.astype(jnp.float32) @ router_w.T
        probs = jax.nn.softmax(logits, axis=-1)
        top_v, top_i = jax.lax.top_k(probs, top_k)
        gates = jax.nn.softmax(top_v, axis=-1)
        comb = jnp.sum(jax.nn.one_hot(top_i, E, dtype=gates.dtype) * gates[..., None], axis=1)
        out = jnp.zeros_like(normed)
        for e in range(E):
            y = _swiglu(normed, gate_up_w[e], down_w[e])
            out = out + comb[:, e, None] * y
        out = out + _swiglu(normed, shared_gate_up_w, shared_down_w)
        return out.reshape(B, S, D)
    x = L0_attn_x
    x = x + 0.5 * _L0_ffn_ref(_layernorm(x, axis=-1), L0_ffn_ln_gamma, L0_ffn_ln_beta, L0_ffn_router_w, L0_ffn_gate_up_w, L0_ffn_down_w, L0_ffn_shared_gate_up_w, L0_ffn_shared_down_w)
    x = x + _L0_attn_ref(_layernorm(x, axis=-1), L0_attn_Wq, L0_attn_bq, L0_attn_Wk, L0_attn_bk, L0_attn_Wv, L0_attn_bv, L0_attn_gamma, L0_attn_beta)
    x = x + 0.5 * _L0_ffn_ref(_layernorm(x, axis=-1), L0_ffn_ln_gamma, L0_ffn_ln_beta, L0_ffn_router_w, L0_ffn_gate_up_w, L0_ffn_down_w, L0_ffn_shared_gate_up_w, L0_ffn_shared_down_w)
    return x

_drawn_inputs = setup_inputs


def setup_inputs(seed=0):
    import zlib

    import numpy as np

    out = dict(_drawn_inputs(seed))
    spreads = {'L0_attn_gamma': (1.0, 0.2),
     'L0_attn_beta': (0.0, 0.1),
     'L0_ffn_ln_gamma': (1.0, 0.2),
     'L0_ffn_ln_beta': (0.0, 0.1)}
    factors = {'L0_attn_bq': 4.704, 'L0_attn_bk': 8.0}
    for name, (base, spread) in spreads.items():
        noise = np.random.default_rng([zlib.crc32(name.encode()), seed]).standard_normal(out[name].shape)
        drawn = base * np.exp(spread * noise) if base else spread * noise
        out[name] = jnp.asarray(drawn.astype(out[name].dtype))
    for name, factor in factors.items():
        out[name] = (out[name] * factor).astype(out[name].dtype)
    return out
```

```python
from contextlib import ExitStack

import concourse.bass as bass
from concourse import mybir

F32 = mybir.dt.float32
BF16 = mybir.dt.bfloat16
I32 = mybir.dt.int32
ALU = mybir.AluOpType
ACT = mybir.ActivationFunctionType
AX_X = mybir.AxisListType.X

P = 128
D = 128
NT = 32
TB = 4
NG = 2
TPG = NT // NG
BPG = TPG // TB
NE = 8
FF = 384
FC = FF // P
REGION = TPG * P
MAXB = 2 * TPG + NE - 1
NBLK = -(-MAXB // 4) * 4
SPARE = NBLK - 2 * TPG
ROWS = NE * REGION + SPARE * P
EPS = 1e-5
SCALE = 128 ** -0.5
SLOPE = 0.01
TAKEN = -3.0e38
TAKEN_BELOW = -2.9e38
RSQRT_SEED = float(0x5F3759DF)
KTOP = 32
NSTEP = 3


def macaron(nc, x, wq, bq, wk, bk, wv, bv, ga, ba, gf, bf, rw, guw, dnw, sguw, sdnw, out, xs, ys):
    ctx = ExitStack()
    with ctx:
        def sb(name, shape, dt=F32):
            return ctx.enter_context(nc.sbuf_tensor(name, shape, dt))

        def sem(name):
            return ctx.enter_context(nc.semaphore(name))

        def bank(name):
            return ctx.enter_context(nc.psum_tensor(name, [P, TB, P], F32))

        ps_g, ps_u, ps_h = bank("ps_g"), bank("ps_u"), bank("ps_h")
        ps_x, ps_y = bank("ps_x"), bank("ps_y")
        w0, w1 = bank("w0"), bank("w1")
        ps_s = bank("ps_s")
        ps_lg = ps_s[:, 0, 0:TB * NE].rearrange("p (t e) -> p t e", e=NE)
        ps_pf = ps_s[:, 1, 0:(TB + 1) * NE].rearrange("p (t e) -> p t e", e=NE)

        def ff(t):
            return t[:, 0:FC, :].rearrange("p c f -> p (c f)")

        ident = sb("ident", [P, P])
        upper = sb("upper", [P, P], BF16)
        ones = sb("ones", [P, P], BF16)
        one_f = sb("one_f", [P, P])
        first_w = sb("first_w", [P, NE])
        region0 = sb("region0", [P, NE])
        full_at = sb("full_at", [P, TPG])
        blk_no = sb("blk_no", [P, NBLK])
        zeros = sb("zeros", [P, 2048])
        ga_b, ba_b, gf_b, bf_b, bv_b = (sb(n, [P, D]) for n in ("ga_b", "ba_b", "gf_b", "bf_b", "bv_b"))
        bq_c, bk_c = sb("bq_c", [P, 1]), sb("bk_c", [P, 1])

        raw_gu = sb("raw_gu", [P, NE, 2 * FC, D])
        raw_dn = sb("raw_dn", [P, NE, FF])
        raw_sm = sb("raw_sm", [P, 6, P])
        raw_rw = sb("raw_rw", [NE, D])
        gu_t = sb("gu_t", [P, NE, 2 * FF])
        dn_t = sb("dn_t", [P, NE, FF])
        sm_t = sb("sm_t", [P, 6, P])
        rw_t = sb("rw_t", [P, NE])
        sg_t, su_t, sd_t, wq_t, wk_t, wv_t = (sm_t[:, n, :] for n in range(6))

        xres = sb("xres", [P, NT, D])
        slots = sb("slots", [P, 2, NT], I32)
        lg_all = sb("lg_all", [P, NT, NE])
        oh_all = [sb(f"oh_all{c}", [P, NT, NE]) for c in range(2)]
        m1_all = sb("m1_all", [P, NT])
        gates = sb("gates", [P, 2, NT])
        run = sb("run", [P, NE])

        bn6 = sb("bn6", [P, TB, 6])
        mv = sb("mv", [P, TB, 2])
        nv, ny, nt = sb("nv", [P, TB]), sb("ny", [P, TB]), sb("nt", [P, TB])
        z = sb("z", [P, TB, D])
        zg = sb("zg", [P, TB, D])
        nz = sb("nz", [P, TB, D])
        nz_t = sb("nz_t", [P, TB, P])
        sel = sb("sel", [P, 2 * TB + 1, NE], BF16)
        pos = sb("pos", [P, TB, NE])
        r8 = sb("r8", [P, TB, NE])
        r8b = sb("r8b", [P, TB, NE])
        f4 = sb("f4", [P, TB])
        s_idx = sb("s_idx", [P, 2, TB], I32)
        sg = sb("sg", [P, TB * P])
        sh = sb("sh", [P, TB, P])
        g_idx = sb("g_idx", [P, 2, TB], I32)
        yg = sb("yg", [P, TB, 2, D])
        x1 = sb("x1", [P, TB, D])
        xn = sb("xn", [P, TB, D])
        xn_t = sb("xn_t", [P, TB, P])
        q_t = sb("q_t", [P, TB, P])
        k_t = sb("k_t", [P, TB, P])
        v = sb("v", [P, TB, D])
        sc = sb("sc", [P, TB, P])
        top = sb("top", [P, TB, KTOP])
        wk_s = sb("wk_s", [P, TB, P])
        nmax = sb("nmax", [P, TB])
        ex = sb("ex", [P, TB, P])
        pr = sb("pr", [P, TB, P])
        psum_p = sb("psum_p", [P, TB])
        rinv = sb("rinv", [P, TB])
        pr_t = sb("pr_t", [P, TB, P])
        o = sb("o", [P, TB, D])
        lr = sb("lr", [P, TB, D])
        rr = sb("rr", [P, TB, D])
        rn = sb("rn", [P, TB, D])
        rg = sb("rg", [P, TB, D])
        x1b = sb("x1b", [P, TB, D])
        fin = sb("fin", [P, TB, D])

        gt = sb("gt", [P, TPG, NE])
        g4 = sb("g4", [P, 6, TPG])
        cnt = sb("cnt", [P, NE])
        nbk = sb("nbk", [P, NE])
        bend = sb("bend", [P, NE])
        shift = sb("shift", [P, NE])
        mv16 = sb("mv16", [P, TPG])
        cmp16 = sb("cmp16", [P, NE, TPG])
        cmpb = sb("cmpb", [P, NBLK, NE])
        cmpb2 = sb("cmpb2", [P, NBLK, NE])
        be = sb("be", [P, NBLK])
        bs = sb("bs", [P, NBLK])
        bt = sb("bt", [P, NBLK])
        tab_w = [sb(f"tab_w{n}", [P, NBLK], I32) for n in range(2 * NG)]
        tab_r = [sb(f"tab_r{n}", [P, NBLK], I32) for n in range(2 * NG)]

        xin = sb("xin", [P, 4, D])
        x_t = sb("x_t", [P, 2, P])
        sil = sb("sil", [P, 2, FF])
        h = sb("h", [P, 2, FF])
        h_t = sb("h_t", [P, 2, FF])
        yb = sb("yb", [P, 2, D])

        ld_c, ld_x, ld_sm = sem("ld_c"), sem("ld_x"), sem("ld_sm")
        ld_gu, ld_dn = sem("ld_gu"), sem("ld_dn")
        cst, pc, zfill, ready_z = sem("cst"), sem("pc"), sem("zfill"), sem("ready_z")
        wt_ps, wt_a, wt_v = sem("wt_ps"), sem("wt_a"), sem("wt_v")
        rt_bn, rt_ag, rt_nw, z_done, zg_done, nz_done = (sem(n) for n in ("rt_bn", "rt_ag", "rt_nw", "z_done", "zg_done", "nz_done"))
        nzT_ps, nzT_sb, lg_ps, lg_sb = (sem(n) for n in ("nzT_ps", "nzT_sb", "lg_ps", "lg_sb"))
        shG, shU, sg_done, shh, shD, xr_done = (sem(n) for n in ("shG", "shU", "sg_done", "shh", "shD", "xr_done"))
        rc, sel_done, pf_ps, scat, slot_cp = (sem(n) for n in ("rc", "sel_done", "pf_ps", "scat", "slot_cp"))
        tl, tl_e, bl, tab, gts, run0 = (sem(n) for n in ("tl", "tl_e", "bl", "tab", "gts", "run0"))
        gi, gath, cb = sem("gi"), sem("gath"), sem("cb")
        at_bn, at_ag, at_nw, xn_done = (sem(n) for n in ("at_bn", "at_ag", "at_nw", "xn_done"))
        xnT_ps, xnT_sb, q_ps, q_sb, k_ps, k_sb, v_ps, v_sb = (sem(n) for n in ("xnT_ps", "xnT_sb", "q_ps", "q_sb", "k_ps", "k_sb", "v_ps", "v_sb"))
        s_ps, tk, nm_done, ex_done, pr_done, ri_done, prT_ps, prT_sb, o_ps, o_sb = (
            sem(n) for n in ("s_ps", "tk", "nm_done", "ex_done", "pr_done", "ri_done", "prT_ps", "prT_sb", "o_ps", "o_sb"))
        lr_done, rr_done, ob_bn, ob_ag, ob_nw, rn_done, rg_done, x1b_done, x2_done = (
            sem(n) for n in ("lr_done", "rr_done", "ob_bn", "ob_ag", "ob_nw", "rn_done", "rg_done", "x1b_done", "x2_done"))
        sc_sb = sem("sc_sb")
        rrow = sem("rrow")
        passed = {e: sem(f"passed_{n}") for e, n in ((nc.vector.engine, "dve"), (nc.gpsimd.engine, "pool"))}
        scat_ok = sem("scat_ok")
        out_st, sm_done = sem("out_st"), sem("sm_done")
        xin_ld = [sem(f"xin_ld{k}") for k in range(4)]
        yst = [sem(f"yst{k}") for k in range(2)]
        xT_ps, xT_sb, g_ps, u_ps, sil_done, h_done, hT_ps, hT_sb, y_ps, y_sb = (
            sem(n) for n in ("xT_ps", "xT_sb", "g_ps", "u_ps", "sil_done", "h_done", "hT_ps", "hT_sb", "y_ps", "y_sb"))

        CREDITS = [(xT_ps, 4), (xT_sb, 2), (u_ps, 2), (sil_done, 2), (h_done, 2), (hT_ps, 2), (hT_sb, 2), (y_ps, 2),
                   (y_sb, 2), (yst[0], 16), (yst[1], 16), (zg_done, 1), (shh, 1), (xr_done, 1), (shU, 1), (shD, 1),
                   (scat_ok, 1), (nzT_ps, 1), (slot_cp, 1),
                   (cb, 2 * TB), (out_st, 16)]

        ctx.enter_context(nc.allow_low_precision(reason="rows' numbers are whole and below 2**24, exact in float32"))
        block = ctx.enter_context(nc.Block())
        N_RT = 2 + 3 * NSTEP
        N_RC = 11
        N_RC2 = 6

        def apart(eng):
            eng.sem_inc(passed[eng.engine], 1)

        @block.sync
        def _(sp):
            for s, n in CREDITS:
                sp.sem_inc(s, n)
            for n in range(BPG * NG):
                sp.dma_start(xres[:, n * TB:(n + 1) * TB, :],
                             x[n * TB:(n + 1) * TB].rearrange("t p d -> p t d")).then_inc(ld_x, 16)
            sp.dma_start(raw_gu[:, 0:NE // 2], guw[0:NE // 2].rearrange("e (c p) d -> p e c d", p=P)).then_inc(ld_gu, 16)
            sp.dma_start(raw_gu[:, NE // 2:], guw[NE // 2:].rearrange("e (c p) d -> p e c d", p=P)).then_inc(ld_gu, 16)
            sp.dma_start(raw_dn[:], dnw.rearrange("e p f -> p e f")).then_inc(ld_dn, 16)

            def load(ph, g, b, m, k):
                row = sp.value_load(tab_r[ph][0:1, bass.ds(b, 1)], min_val=0, max_val=ROWS - P)
                sp.wait_ge(xT_ps, ph * NBLK + b + 1)
                sp.dma_start(xin[:, k, :], xs[g][bass.ds(row, P), :]).then_inc(xin_ld[k], 16)

            def store(ph, g, b, k):
                sp.wait_ge(y_sb, ph * NBLK + b + 3)
                sp.dma_start(ys[g][bass.ds(b * P, P), :], yb[:, k, :]).then_inc(yst[k], 16)

            def blocks(ph, g):
                sp.wait_ge(tab, ph + 1)
                sp.wait_ge(scat, 2 * TB * 16 * (ph + 1) * BPG)
                def slot(b, q):
                    if not isinstance(b, int) or b + 3 < NBLK:
                        load(ph, g, b + 3, None, (q + 3) % 4)
                    if not isinstance(b, int) or b >= 2:
                        store(ph, g, b - 2, q % 2)
                for b in range(3):
                    load(ph, g, b, None, b)
                for b in range(4):
                    slot(b, b)
                with sp.Fori(0, NBLK // 4 - 2) as i:
                    for q in range(4):
                        slot(i * 4 + (4 + q), q)
                for b in range(NBLK - 4, NBLK + 2):
                    slot(b, b % 4)

            for g in range(NG):
                blocks(g, g)
            for g in range(NG):
                blocks(NG + g, g)
            for g in range(NG):
                with sp.Fori(0, BPG) as i:
                    sp.wait_ge(cb, 2 * TB * (i + (NG * BPG + g * BPG + 2)))
                    sp.dma_start(out[bass.ds(i * TB + g * TPG, TB)].rearrange("t p d -> p t d"), fin[:]).then_inc(out_st, 16)
            sp.wait_ge(out_st, 16 * (1 + NG * BPG))
            for k in range(2):
                sp.wait_ge(yst[k], 16 * (1 + 2 * NG * NBLK // 2))

        @block.tensor
        def _(pe):
            pe.wait_ge(cst, 1)
            pe.wait_ge(ld_sm, 16 * 6)
            for n in range(3):
                pe.transpose(w0[:, n, :], raw_sm[:, n, :], ident[:])
            for n in range(3):
                pe.transpose(w1[:, n, :], raw_sm[:, 3 + n, :], ident[:])
            pe.transpose(ps_lg[:, 0, :], raw_rw[:], ident[0:NE, 0:NE]).then_inc(wt_ps, 1)
            pe.wait_ge(ld_dn, 16)
            pe.wait_ge(ld_gu, 32)
            for e in range(NE):
                if e >= 1:
                    pe.wait_ge(wt_a, 2 * e + 1)
                if e >= 2:
                    pe.wait_ge(wt_v, e)
                for c in range(FC):
                    pe.transpose((ps_g, ps_x)[e % 2][:, c, :], raw_gu[:, e, c, :], ident[:])
                for c in range(FC):
                    pe.transpose((ps_u, ps_y)[e % 2][:, c, :], raw_gu[:, e, FC + c, :], ident[:])
                for c in range(FC):
                    t = pe.transpose(ps_h[:, c, :], raw_dn[:, e, c * P:(c + 1) * P], ident[:])
                t.then_inc(wt_ps, 1)
            pe.wait_ge(wt_a, 1 + 2 * NE)
            pe.wait_ge(wt_v, 1 + NE)

            def route(R, after_attention=None):
                pe.wait_ge(nz_done, R + 1)
                pe.wait_ge(shh, R + 1)
                if after_attention is not None:
                    pe.wait_ge(prT_sb, after_attention + 1)
                for k in range(TB):
                    t = pe.transpose(w1[:, k, :], nz[:, k, :], ident[:])
                t.then_inc(nzT_ps, 1)
                pe.wait_ge(nzT_sb, R + 1)
                for k in range(TB):
                    t = pe.matmul(ps_lg[:, k, :], nz_t[:, k, :], rw_t[:], start=True, stop=True)
                t.then_inc(lg_ps, 1)
                pe.wait_ge(xr_done, R + 1)
                if after_attention is not None:
                    pe.wait_ge(o_sb, TB * (after_attention + 1))
                pe.matmul(w0[:], sg_t, nz_t[:], start=True, stop=True).then_inc(shG, 1)
                pe.matmul(w1[:], su_t, nz_t[:], start=True, stop=True).then_inc(shU, 1)
                pe.wait_ge(sel_done, R + 1)
                pe.matmul(ps_pf, upper[:], sel[:, TB:, :], start=True, stop=False)
                for n in range(1, TB + 1):
                    t = pe.matmul(ps_pf, ones[:], sel[:, TB - n:2 * TB + 1 - n, :], start=False, stop=(n == TB))
                t.then_inc(pf_ps, 1)
                pe.wait_ge(shh, R + 2)
                for k in range(TB):
                    t = pe.matmul(w0[:, k, :], sh[:, k, :], sd_t, start=True, stop=True)
                t.then_inc(shD, 1)

            def attention(A):
                pe.wait_ge(xn_done, TB * (A + 1))
                pe.wait_ge(xr_done, A + (NG * BPG + 1))
                for k in range(TB):
                    t = pe.transpose(w0[:, k, :], xn[:, k, :], ident[:])
                t.then_inc(xnT_ps, 1)
                pe.wait_ge(xnT_sb, A + 1)
                pe.wait_ge(shh, A + (NG * BPG + 1))
                pe.matmul(w1[:], wq_t, xn_t[:], start=True, stop=True).then_inc(q_ps, 1)
                pe.matmul(w0[:], wk_t, xn_t[:], start=True, stop=True).then_inc(k_ps, 1)
                pe.wait_ge(q_sb, A + 1)
                for k in range(TB):
                    t = pe.matmul(w1[:, k, :], xn_t[:, k, :], wv_t, start=True, stop=True)
                t.then_inc(v_ps, 1)
                pe.wait_ge(k_sb, A + 1)
                for k in range(TB):
                    t = pe.matmul(w0[:, k, :], q_t[:, k, :], k_t[:, k, :], start=True, stop=True)
                t.then_inc(s_ps, 1)
                pe.wait_ge(v_sb, A + 1)
                pe.wait_ge(pr_done, TB * (A + 1))
                for k in range(TB):
                    t = pe.transpose(w1[:, k, :], pr[:, k, :], ident[:])
                t.then_inc(prT_ps, 1)
                pe.wait_ge(prT_sb, A + 1)
                for k in range(TB):
                    t = pe.matmul(w0[:, k, :], pr_t[:, k, :], v[:, k, :], start=True, stop=True)
                t.then_inc(o_ps, 1)

            def blocks(ph):
                def slot(b, q):
                    static = isinstance(b, int)
                    B = b + ph * NBLK
                    k = q % 2
                    if not static or b + 1 < NBLK:
                        k4 = (q + 1) % 4
                        pe.wait_ge(xin_ld[k4], (B + (1 - k4 + 4)) * 4)
                        pe.wait_ge(xT_sb, B + 3)
                        pe.transpose(ps_x[:, 0, :], xin[:, k4, :], ident[:]).then_inc(xT_ps, 1)
                    if not static or b < NBLK:
                        off = pe.value_load(tab_w[ph][0:1, bass.ds(b, 1)], min_val=0, max_val=(NE - 1) * FF)
                        pe.wait_ge(xT_sb, B + 3)
                        pe.wait_ge(sil_done, B + 2)
                        gu = gu_t[:].rearrange("p e f -> p (e f)")
                        pe.matmul(ff(ps_g), x_t[:, k, :], gu[:, bass.ds(off * 2, FF)], start=True, stop=True).then_inc(g_ps, 1)
                        pe.wait_ge(h_done, B + 2)
                        pe.matmul(ff(ps_u), x_t[:, k, :], gu[:, bass.ds(off * 2 + FF, FF)], start=True, stop=True).then_inc(u_ps, 1)
                    if not static or 2 <= b:
                        off = pe.value_load(tab_w[ph][0:1, bass.ds(b - 2, 1)], min_val=0, max_val=(NE - 1) * FF)
                        pe.wait_ge(hT_sb, B + 1)
                        pe.wait_ge(y_sb, B)
                        dn = dn_t[:].rearrange("p e f -> p (e f)")
                        for c in range(FC):
                            t = pe.matmul(ps_y[:, 0, :], h_t[:, k, c * P:(c + 1) * P], dn[:, bass.ds(off + c * D, D)],
                                          start=(c == 0), stop=(c == FC - 1))
                        t.then_inc(y_ps, 1)
                    if not static or 1 <= b <= NBLK:
                        pe.wait_ge(h_done, B + 2)
                        pe.wait_ge(hT_sb, B + 1)
                        for c in range(FC):
                            t = pe.transpose(ps_h[:, c, :], h[:, 1 - k, c * P:(c + 1) * P], ident[:])
                        t.then_inc(hT_ps, 1)

                pe.wait_ge(tab, ph + 1)
                pe.wait_ge(xin_ld[0], (ph * (NBLK // 4) + 1) * 16)
                pe.wait_ge(xT_sb, ph * NBLK + 2)
                pe.transpose(ps_x[:, 0, :], xin[:, 0, :], ident[:]).then_inc(xT_ps, 1)
                for b in range(4):
                    slot(b, b)
                with pe.Fori(0, NBLK // 4 - 2) as i:
                    for q in range(4):
                        slot(i * 4 + (4 + q), q)
                for b in range(NBLK - 4, NBLK + 2):
                    slot(b, b % 4)

            for g in range(NG):
                with pe.Fori(0, BPG) as i:
                    route(i + g * BPG)
            for g in range(NG):
                blocks(g)
            for g in range(NG):
                with pe.Fori(0, BPG) as i:
                    attention(i + g * BPG)
                    route(i + (NG + g) * BPG, i + g * BPG)
            for g in range(NG):
                blocks(NG + g)

        @block.scalar
        def _(act):
            act.dma_start(raw_sm[:, 0:2, :], sguw.rearrange("(c p) d -> p c d", p=P)).then_inc(ld_sm, 16)
            for n, w in enumerate((sdnw, wq, wk, wv)):
                act.dma_start(raw_sm[:, 2 + n, :], w).then_inc(ld_sm, 16)
            act.dma_start(raw_rw[:], rw).then_inc(ld_sm, 16)
            for t, w in ((ga_b, ga), (ba_b, ba), (gf_b, gf), (bf_b, bf), (bv_b, bv)):
                act.dma_start(t[:], w.partition_broadcast(P)).then_inc(ld_c, 16)
            for t, w in ((bq_c, bq), (bk_c, bk)):
                act.dma_start(t[:], w.rearrange("(p o) -> p o", o=1)).then_inc(ld_c, 16)
            act.wait_ge(ready_z, 1)
            for g in range(NG):
                for n in range(0, ROWS, 16 * P):
                    m = min(16 * P, ROWS - n) // P
                    act.dma_start(xs[g][n:n + m * P].rearrange("(p r) d -> p (r d)", p=P), zeros[:, 0:m * D]).then_inc(zfill, 16)

            act.wait_ge(wt_ps, 1)
            act.copy(sm_t[:, 0:3, :], w0[:, 0:3, :]).then_inc(wt_a, 1)
            for e in range(NE):
                act.wait_ge(wt_ps, 2 + e)
                act.copy(gu_t[:, e, 0:FF], ff((ps_g, ps_x)[e % 2])).then_inc(wt_a, 1)
                act.copy(dn_t[:, e, :], ff(ps_h)).then_inc(wt_a, 1)

            def route(R, tile):
                act.wait_ge(nzT_ps, R + 2)
                act.wait_ge(shU, R + 1)
                act.copy(nz_t[:], w1[:]).then_inc(nzT_sb, 1)
                act.wait_ge(lg_ps, R + 1)
                act.copy(lg_all[:, bass.ds(tile, TB), :], ps_lg).then_inc(lg_sb, 1)
                act.wait_ge(shG, R + 1)
                act.wait_ge(shh, R + 1)
                act.activation(sg[:], w0[:].rearrange("p t d -> p (t d)"), ACT.Silu).then_inc(sg_done, 1)

            def tail(ph):
                act.wait_ge(tl, ph * 9 + 1)
                act.activation(gt[:], gt[:], ACT.Exp).then_inc(tl_e, 1)
                act.wait_ge(tl, ph * 9 + 7)
                act.activation(g4[:, 4, :], g4[:, 3, :], ACT.Exp).then_inc(tl_e, 1)

            def attention(A):
                act.wait_ge(xnT_ps, A + 1)
                act.copy(xn_t[:], w0[:]).then_inc(xnT_sb, 1)
                act.wait_ge(q_ps, A + 1)
                act.activation(q_t[:], w1[:], ACT.Identity, bias=bq_c[:]).then_inc(q_sb, 1)
                act.wait_ge(k_ps, A + 1)
                act.activation(k_t[:], w0[:], ACT.Identity, bias=bk_c[:]).then_inc(k_sb, 1)
                act.wait_ge(s_ps, A + 1)
                act.copy(sc[:], w0[:]).then_inc(sc_sb, 1)
                act.wait_ge(nm_done, A + 1)
                for k in range(TB):
                    act.activation(ex[:, k, :], sc[:, k, :], ACT.Exp, bias=nmax[:, k:k + 1], scale=SCALE).then_inc(ex_done, 1)
                act.wait_ge(prT_ps, A + 1)
                act.copy(pr_t[:], w1[:]).then_inc(prT_sb, 1)
                act.wait_ge(o_ps, A + 1)
                act.wait_ge(ri_done, A + 1)
                for k in range(TB):
                    act.activation(o[:, k, :], w0[:, k, :], ACT.Copy, scale=rinv[:, k:k + 1]).then_inc(o_sb, 1)

            def blocks(ph):
                def slot(b, q):
                    static = isinstance(b, int)
                    B = b + ph * NBLK
                    k = q % 2
                    if not static or b < NBLK:
                        act.wait_ge(g_ps, B + 1)
                        act.wait_ge(h_done, B + 1)
                        act.activation(sil[:, k, :], ff(ps_g), ACT.Silu).then_inc(sil_done, 1)
                    if not static or b >= 2:
                        act.wait_ge(y_ps, B + 1)
                        act.wait_ge(yst[k], (B - k) * 8)
                        act.copy(yb[:, k, :], ps_y[:, 0, :]).then_inc(y_sb, 1)
                    if not static or 1 <= b <= NBLK:
                        act.wait_ge(hT_ps, B + 2)
                        act.wait_ge(y_ps, B)
                        act.copy(h_t[:, 1 - k, :], ff(ps_h)).then_inc(hT_sb, 1)
                for b in range(4):
                    slot(b, b)
                with act.Fori(0, NBLK // 4 - 2) as i:
                    for q in range(4):
                        slot(i * 4 + (4 + q), q)
                for b in range(NBLK - 4, NBLK + 2):
                    slot(b, b % 4)

            for g in range(NG):
                with act.Fori(0, BPG) as i:
                    route(i + g * BPG, i * TB + g * TPG)
                tail(g)
            for g in range(NG):
                blocks(g)
            for g in range(NG):
                with act.Fori(0, BPG) as i:
                    attention(i + g * BPG)
                    route(i + (NG + g) * BPG, i * TB + g * TPG)
                tail(NG + g)
            for g in range(NG):
                blocks(NG + g)

        @block.vector
        def _(dve):
            dve.memset(zeros[:], 0.0).then_inc(ready_z, 1)
            dve.wait_ge(wt_ps, 1)
            dve.tensor_copy(sm_t[:, 3:6, :], w1[:, 0:3, :])
            dve.tensor_copy(rw_t[:], ps_lg[:, 0, :]).then_inc(wt_v, 1)
            for e in range(NE):
                dve.wait_ge(wt_ps, 2 + e)
                dve.tensor_copy(gu_t[:, e, FF:2 * FF], ff((ps_u, ps_y)[e % 2])).then_inc(wt_v, 1)
            dve.wait_ge(cst, 1)
            dve.wait_ge(ld_c, 16 * 7)
            dve.wait_ge(ld_x, 16 * NG * BPG)

            def rsqrt(chain, at, mult, add):
                n = [0]

                def link(ins):
                    n[0] += 1
                    ins.then_inc(chain, 1)
                    dve.wait_ge(chain, at + n[0])
                link(dve.tensor_scalar(nv[:], mv[:, :, 1], mult, add, ALU.mult, ALU.add))
                link(dve.tensor_scalar(ny[:].bitcast(I32), nv[:].bitcast(I32), -0.5, RSQRT_SEED, ALU.mult, ALU.add))
                for _ in range(NSTEP):
                    link(dve.scalar_tensor_tensor(nt[:], ny[:], -0.5, ny[:], ALU.mult, ALU.mult))
                    link(dve.tensor_tensor(nt[:], nt[:], nv[:], ALU.mult))
                    link(dve.scalar_tensor_tensor(ny[:], nt[:], 1.5, ny[:], ALU.add, ALU.mult))
                assert n[0] == N_RT

            def stats(src, bn, ag, at):
                for k in range(TB):
                    dve.bn_stats(bn6[:, k, :], src(k)).then_inc(bn, 1)
                for k in range(TB):
                    dve.wait_ge(bn, at + k + 1)
                    apart(dve)
                    dve.bn_aggr(mv[:, k, :], bn6[:, k, :]).then_inc(ag, 1)
                dve.wait_ge(ag, at + TB)

            def bc(t):
                return t.rearrange("p (t o) -> p t o", o=1).broadcast_to([P, TB, NE])

            def route(R, tile):
                stats(lambda k: xres[:, bass.ds(tile + k, 1), :].rearrange("p t d -> p (t d)"), rt_bn, rt_ag, R * TB)
                rsqrt(rt_nw, R * N_RT, 1.0 + EPS, EPS * EPS)
                dve.wait_ge(zg_done, R + 1)
                for k in range(TB):
                    dve.tensor_scalar(z[:, k, :], xres[:, bass.ds(tile + k, 1), :].rearrange("p t d -> p (t d)"),
                                      mv[:, k, 0:1], ny[:, k:k + 1], ALU.subtract, ALU.mult).then_inc(z_done, 1)
                n = [0]

                def link(ins):
                    n[0] += 1
                    ins.then_inc(rc, 1)
                    dve.wait_ge(rc, R * (N_RC + N_RC2) + n[0])
                fw = first_w[:].rearrange("p (o e) -> p o e", o=1).broadcast_to([P, TB, NE])
                lg = lg_all[:, bass.ds(tile, TB), :]
                m1 = m1_all[:, bass.ds(tile, TB)]
                oh1 = oh_all[0][:, bass.ds(tile, TB), :]
                oh2 = oh_all[1][:, bass.ds(tile, TB), :]
                dve.wait_ge(lg_sb, R + 1)
                link(dve.tensor_reduce(m1, lg, AX_X, ALU.max))
                link(dve.tensor_tensor(r8[:], lg, bc(m1), ALU.is_equal))
                link(dve.tensor_tensor(r8[:], r8[:], fw, ALU.mult))
                link(dve.tensor_reduce(f4[:], r8[:], AX_X, ALU.max))
                link(dve.tensor_tensor(oh1, fw, bc(f4[:]), ALU.is_equal))
                link(dve.scalar_tensor_tensor(r8b[:], oh1, TAKEN, lg, ALU.mult, ALU.add))
                link(dve.tensor_reduce(f4[:], r8b[:], AX_X, ALU.max))
                link(dve.tensor_tensor(r8[:], r8b[:], bc(f4[:]), ALU.is_equal))
                link(dve.tensor_tensor(r8[:], r8[:], fw, ALU.mult))
                link(dve.tensor_reduce(f4[:], r8[:], AX_X, ALU.max))
                link(dve.tensor_tensor(oh2, fw, bc(f4[:]), ALU.is_equal))
                dve.tensor_tensor(sel[:, TB:2 * TB, :], oh1, oh2, ALU.add).then_inc(sel_done, 1)
                assert n[0] == N_RC
                dve.wait_ge(shU, R + 2)
                dve.wait_ge(sg_done, R + 1)
                dve.wait_ge(shD, R + 1)
                dve.tensor_tensor(sh[:].rearrange("p t d -> p (t d)"), sg[:], w1[:].rearrange("p t d -> p (t d)"),
                                  ALU.mult).then_inc(shh, 1)
                dve.wait_ge(pf_ps, R + 1)
                dve.wait_ge(slot_cp, R + 1)
                link(dve.tensor_tensor(pos[:], ps_pf[:, 0:TB, :], run[:].rearrange("p (o e) -> p o e", o=1).broadcast_to([P, TB, NE]), ALU.add))
                link(dve.tensor_tensor(run[:], run[:], ps_pf[:, TB, :], ALU.add))
                link(dve.tensor_tensor(r8[:], oh1, pos[:], ALU.mult))
                dve.wait_ge(scat_ok, R + 1)
                link(dve.tensor_reduce(s_idx[:, 0, :], r8[:], AX_X, ALU.add))
                link(dve.tensor_tensor(r8b[:], oh2, pos[:], ALU.mult))
                link(dve.tensor_reduce(s_idx[:, 1, :], r8b[:], AX_X, ALU.add))
                assert n[0] == N_RC + N_RC2
                dve.wait_ge(shD, R + 2)
                xr = xres[:, bass.ds(tile, TB), :]
                dve.scalar_tensor_tensor(xr, w0[:], 0.5, xr, ALU.mult, ALU.add).then_inc(xr_done, 1)

            def tail(ph, g):
                n = [0]
                N = 9

                def link(ins):
                    n[0] += 1
                    ins.then_inc(tl, 1)
                    dve.wait_ge(tl, ph * N + n[0])
                t0, t1 = g * TPG, (g + 1) * TPG
                m1 = m1_all[:, t0:t1].rearrange("p (t o) -> p t o", o=1).broadcast_to([P, TPG, NE])
                link(dve.tensor_tensor(gt[:], lg_all[:, t0:t1, :], m1, ALU.subtract))
                dve.wait_ge(tl_e, 2 * ph + 1)
                link(dve.tensor_reduce(g4[:, 0, :], gt[:], AX_X, ALU.add))
                link(dve.tensor_tensor(gt[:], gt[:], oh_all[1][:, t0:t1, :], ALU.mult))
                link(dve.tensor_reduce(g4[:, 1, :], gt[:], AX_X, ALU.add))
                link(dve.reciprocal(g4[:, 2, :], g4[:, 0, :]))
                link(dve.tensor_scalar(g4[:, 1, :], g4[:, 1, :], 1.0, None, ALU.subtract))
                link(dve.tensor_tensor(g4[:, 3, :], g4[:, 1, :], g4[:, 2, :], ALU.mult))
                dve.wait_ge(tl_e, 2 * ph + 2)
                link(dve.tensor_scalar(g4[:, 5, :], g4[:, 4, :], 2.0, 2.0, ALU.mult, ALU.add))
                link(dve.reciprocal(gates[:, 0, t0:t1], g4[:, 5, :]))
                assert n[0] == N
                dve.tensor_tensor(gates[:, 1, t0:t1], gates[:, 0, t0:t1], g4[:, 4, :], ALU.mult).then_inc(gts, 1)

            def block_list(ph):
                n = [0]
                N = 14

                def link(ins):
                    n[0] += 1
                    ins.then_inc(bl, 1)
                    dve.wait_ge(bl, ph * N + n[0])
                bn = blk_no[:].rearrange("p (b o) -> p b o", o=1).broadcast_to([P, NBLK, NE])
                link(dve.tensor_tensor(cnt[:], run[:], region0[:], ALU.subtract))
                link(dve.tensor_tensor(cmp16[:], cnt[:].rearrange("p (e o) -> p e o", o=1).broadcast_to([P, NE, TPG]),
                                       full_at[:].rearrange("p (o t) -> p o t", o=1).broadcast_to([P, NE, TPG]), ALU.is_gt))
                link(dve.tensor_reduce(nbk[:], cmp16[:], AX_X, ALU.add))
                link(dve.tensor_tensor_scan(bend[:], one_f[:, 0:NE], nbk[:], 0.0, ALU.mult, ALU.add))
                link(dve.tensor_tensor(cmpb[:], bn, bend[:].rearrange("p (o e) -> p o e", o=1).broadcast_to([P, NBLK, NE]), ALU.is_ge))
                link(dve.tensor_reduce(be[:], cmpb[:], AX_X, ALU.add))
                link(dve.tensor_tensor(cmpb2[:], cmpb[:], nbk[:].rearrange("p (o e) -> p o e", o=1).broadcast_to([P, NBLK, NE]), ALU.mult))
                link(dve.tensor_reduce(bs[:], cmpb2[:], AX_X, ALU.add))
                link(dve.tensor_tensor(bt[:], blk_no[:], bs[:], ALU.subtract))
                link(dve.tensor_scalar(bt[:], bt[:], float(P), None, ALU.mult))
                link(dve.scalar_tensor_tensor(tab_r[ph][:], be[:], float(REGION), bt[:], ALU.mult, ALU.add))
                link(dve.tensor_scalar(be[:], be[:], float(NE - 1), None, ALU.min))
                link(dve.tensor_tensor(shift[:], bend[:], nbk[:], ALU.subtract))
                link(dve.scalar_tensor_tensor(shift[:], shift[:], float(P), region0[:], ALU.mult, ALU.subtract))
                assert n[0] == N
                dve.tensor_scalar(tab_w[ph][:], be[:], float(FF), None, ALU.mult).then_inc(tab, 1)

            def result_rows(ph, g):
                n = [0]

                def link(ins):
                    n[0] += 1
                    ins.then_inc(rrow, 1)
                    dve.wait_ge(rrow, ph * 6 + n[0])
                t0, t1 = g * TPG, (g + 1) * TPG
                dve.wait_ge(slot_cp, (ph + 1) * BPG + 1)
                for c in range(2):
                    link(dve.tensor_tensor(gt[:], oh_all[c][:, t0:t1, :], shift[:].rearrange("p (o e) -> p o e", o=1).broadcast_to([P, TPG, NE]), ALU.mult))
                    link(dve.tensor_reduce(mv16[:], gt[:], AX_X, ALU.add))
                    link(dve.tensor_tensor(slots[:, c, t0:t1], slots[:, c, t0:t1], mv16[:], ALU.add))

            def start_group(ph):
                dve.tensor_copy(run[:], region0[:]).then_inc(run0, 1)
                dve.wait_ge(run0, ph + 1)

            def combine(C, tile, dst):
                dve.wait_ge(gath, 2 * TB * 16 * (C + 1))
                for k in range(TB):
                    xk = xres[:, bass.ds(tile + k, 1), :].rearrange("p t d -> p (t d)")
                    dve.scalar_tensor_tensor(dst[:, k, :], yg[:, k, 0, :], gates[:, 0, bass.ds(tile + k, 1)], xk,
                                             ALU.mult, ALU.add).then_inc(cb, 1)
                for k in range(TB):
                    dve.wait_ge(cb, 2 * TB * (C + 1) + k + 1)
                    dve.scalar_tensor_tensor(dst[:, k, :], yg[:, k, 1, :], gates[:, 1, bass.ds(tile + k, 1)], dst[:, k, :],
                                             ALU.mult, ALU.add).then_inc(cb, 1)

            def attention(A, tile):
                dve.wait_ge(cb, 2 * TB * (A + 2))
                apart(dve)
                stats(lambda k: x1[:, k, :], at_bn, at_ag, A * TB)
                rsqrt(at_nw, A * N_RT, 1.0, EPS)
                for k in range(TB):
                    dve.tensor_scalar(xn[:, k, :], x1[:, k, :], mv[:, k, 0:1], ny[:, k:k + 1],
                                      ALU.subtract, ALU.mult).then_inc(xn_done, 1)
                dve.wait_ge(v_ps, A + 1)
                dve.tensor_tensor(v[:], w1[:], bv_b[:].rearrange("p (o d) -> p o d", o=1).broadcast_to([P, TB, D]), ALU.add).then_inc(v_sb, 1)
                dve.wait_ge(sc_sb, A + 1)
                apart(dve)
                N = 2 * TB * (KTOP // 8)
                for r in range(KTOP // 8):
                    for k in range(TB):
                        if r:
                            dve.wait_ge(tk, A * N + 2 * TB * (r - 1) + TB + k + 1)
                        apart(dve)
                        dve.max(top[:, k, 8 * r:8 * r + 8], wk_s[:, k, :] if r else sc[:, k, :]).then_inc(tk, 1)
                    for k in range(TB):
                        dve.wait_ge(tk, A * N + 2 * TB * r + k + 1)
                        apart(dve)
                        dve.match_replace(wk_s[:, k, :], top[:, k, 8 * r:8 * r + 8], wk_s[:, k, :] if r else sc[:, k, :], TAKEN).then_inc(tk, 1)
                    if r == 0:
                        dve.tensor_scalar(nmax[:], top[:, :, 0], -SCALE, None, ALU.mult).then_inc(nm_done, 1)
                for k in range(TB):
                    dve.wait_ge(tk, A * N + N - TB + k + 1)
                    dve.wait_ge(ex_done, A * TB + k + 1)
                    dve.scalar_tensor_tensor(pr[:, k, :], wk_s[:, k, :], TAKEN_BELOW, ex[:, k, :], ALU.is_lt, ALU.mult).then_inc(pr_done, 1)
                dve.wait_ge(pr_done, TB * (A + 1))
                dve.tensor_reduce(psum_p[:], pr[:], AX_X, ALU.add).then_inc(sm_done, 1)
                dve.wait_ge(sm_done, A + 1)
                dve.reciprocal(rinv[:], psum_p[:]).then_inc(ri_done, 1)
                dve.wait_ge(o_sb, TB * (A + 1))
                dve.scalar_tensor_tensor(lr[:], o[:], SLOPE, o[:], ALU.mult, ALU.max).then_inc(lr_done, 1)
                dve.wait_ge(rr_done, A + 1)
                apart(dve)
                stats(lambda k: rr[:, k, :], ob_bn, ob_ag, A * TB)
                rsqrt(ob_nw, A * N_RT, 1.0, EPS)
                for k in range(TB):
                    dve.tensor_scalar(rn[:, k, :], rr[:, k, :], mv[:, k, 0:1], ny[:, k:k + 1],
                                      ALU.subtract, ALU.mult).then_inc(rn_done, 1)
                dve.wait_ge(x2_done, A + 1)
                apart(dve)

            def blocks(ph):
                def slot(b, q):
                    static = isinstance(b, int)
                    B = b + ph * NBLK
                    k = q % 2
                    if not static or b + 1 < NBLK:
                        dve.wait_ge(xT_ps, B + 6)
                        dve.wait_ge(u_ps, B + 2)
                        dve.tensor_copy(x_t[:, 1 - k, :], ps_x[:, 0, :]).then_inc(xT_sb, 1)
                    if not static or b < NBLK:
                        dve.wait_ge(u_ps, B + 3)
                        dve.wait_ge(sil_done, B + 3)
                        dve.wait_ge(hT_ps, B + 1)
                        dve.tensor_tensor(h[:, k, :], sil[:, k, :], ff(ps_u), ALU.mult).then_inc(h_done, 1)
                dve.wait_ge(xT_ps, ph * NBLK + 5)
                dve.wait_ge(u_ps, ph * NBLK + 1)
                dve.tensor_copy(x_t[:, 0, :], ps_x[:, 0, :]).then_inc(xT_sb, 1)
                for b in range(4):
                    slot(b, b)
                with dve.Fori(0, NBLK // 4 - 2) as i:
                    for q in range(4):
                        slot(i * 4 + (4 + q), q)
                for b in range(NBLK - 4, NBLK + 2):
                    slot(b, b % 4)

            for g in range(NG):
                start_group(g)
                with dve.Fori(0, BPG) as i:
                    route(i + g * BPG, i * TB + g * TPG)
                block_list(g)
                tail(g, g)
                result_rows(g, g)
            for g in range(NG):
                blocks(g)
            for g in range(NG):
                dve.wait_ge(gts, g + 1)
                start_group(NG + g)
                with dve.Fori(0, BPG) as i:
                    combine(i + g * BPG, i * TB + g * TPG, x1)
                    attention(i + g * BPG, i * TB + g * TPG)
                    route(i + (NG + g) * BPG, i * TB + g * TPG)
                block_list(NG + g)
                tail(NG + g, g)
                result_rows(NG + g, g)
            for g in range(NG):
                blocks(NG + g)
            for g in range(NG):
                dve.wait_ge(gts, NG + g + 1)
                with dve.Fori(0, BPG) as i:
                    dve.wait_ge(out_st, 16 * (i + (g * BPG + 1)))
                    combine(i + (NG + g) * BPG, i * TB + g * TPG, fin)

        @block.gpsimd
        def _(pool):
            pool.memset(sel[:], 0.0).then_inc(pc, 1)
            pool.memset(one_f[:], 1.0).then_inc(pc, 1)
            pool.memset(ones[:], 1.0).then_inc(pc, 1)
            pool.wait_ge(pc, 3)
            pool.affine_select(out=ident[:], in_=one_f[:], compare_op=ALU.is_equal, fill=0.0, base=0,
                               pattern=[[-1, P]], channel_multiplier=1)
            pool.affine_select(out=upper[:], in_=ones[:], compare_op=ALU.is_ge, fill=0.0, base=-1,
                               pattern=[[1, P]], channel_multiplier=-1)
            pool.iota(first_w[:], pattern=[[-1, NE]], base=NE, channel_multiplier=0, allow_small_or_imprecise_dtypes=True)
            pool.iota(region0[:], pattern=[[REGION, NE]], base=0, channel_multiplier=0, allow_small_or_imprecise_dtypes=True)
            pool.iota(full_at[:], pattern=[[P, TPG]], base=0, channel_multiplier=0, allow_small_or_imprecise_dtypes=True)
            pool.iota(blk_no[:], pattern=[[1, NBLK]], base=0, channel_multiplier=0,
                      allow_small_or_imprecise_dtypes=True).then_inc(pc, 1)
            pool.wait_ge(pc, 4)
            pool.nop().then_inc(cst, 1)
            pool.wait_ge(ld_c, 16 * 7)
            pool.wait_ge(zfill, 16 * NG * (-(-ROWS // (16 * P))))

            def wide(t):
                return t[:].rearrange("p (o d) -> p o d", o=1).broadcast_to([P, TB, D])

            def route(R, tile, g):
                pool.wait_ge(z_done, TB * (R + 1))
                pool.tensor_tensor(zg[:], z[:], wide(gf_b), ALU.mult).then_inc(zg_done, 1)
                pool.wait_ge(zg_done, R + 2)
                pool.wait_ge(nzT_ps, R + 1)
                pool.wait_ge(scat_ok, R + 1)
                pool.tensor_tensor(nz[:], zg[:], wide(bf_b), ALU.add).then_inc(nz_done, 1)
                pool.wait_ge(rc, (R + 1) * (N_RC + N_RC2))
                apart(pool)
                pool.tensor_copy(slots[:, :, bass.ds(tile, TB)], s_idx[:]).then_inc(slot_cp, 1)
                pool.wait_ge(nz_done, R + 1)
                apart(pool)
                for k in range(TB):
                    for c in range(2):
                        pool.indirect_dma_start(xs[g], bass.IndirectOffsetOnAxis(s_idx[:, c, k:k + 1], 0),
                                                nz[:, k, :], None).then_inc(scat, 16)
                pool.wait_ge(scat, 2 * TB * 16 * (R + 1))
                pool.sem_inc(scat_ok, 1)

            def gather(C, tile, g):
                pool.wait_ge(cb, 2 * TB * (C + 1))
                apart(pool)
                pool.tensor_copy(g_idx[:], slots[:, :, bass.ds(tile, TB)]).then_inc(gi, 1)
                pool.wait_ge(gi, C + 1)
                apart(pool)
                for k in range(TB):
                    for c in range(2):
                        pool.indirect_dma_start(yg[:, k, c, :], None, ys[g],
                                                bass.IndirectOffsetOnAxis(g_idx[:, c, k:k + 1], 0)).then_inc(gath, 16)

            def attention(A, tile):
                pool.wait_ge(cb, 2 * TB * (A + 2))
                pool.tensor_tensor(x1b[:], x1[:], wide(ba_b), ALU.add).then_inc(x1b_done, 1)
                pool.wait_ge(lr_done, A + 1)
                pool.tensor_tensor(rr[:], lr[:], xn[:], ALU.add).then_inc(rr_done, 1)
                pool.wait_ge(rn_done, TB * (A + 1))
                pool.tensor_tensor(rg[:], rn[:], wide(ga_b), ALU.mult).then_inc(rg_done, 1)
                pool.wait_ge(rg_done, A + 1)
                pool.wait_ge(x1b_done, A + 1)
                pool.tensor_tensor(xres[:, bass.ds(tile, TB), :], rg[:], x1b[:], ALU.add).then_inc(x2_done, 1)

            def stored(ph):
                pool.wait_ge(rrow, 6 * (ph + 1))
                for k in range(2):
                    pool.wait_ge(yst[k], 16 * (1 + (ph + 1) * NBLK // 2))

            for g in range(NG):
                with pool.Fori(0, BPG) as i:
                    route(i + g * BPG, i * TB + g * TPG, g)
            for g in range(NG):
                stored(g)
                with pool.Fori(0, BPG) as i:
                    gather(i + g * BPG, i * TB + g * TPG, g)
                    attention(i + g * BPG, i * TB + g * TPG)
                    route(i + (NG + g) * BPG, i * TB + g * TPG, g)
            for g in range(NG):
                stored(NG + g)
                with pool.Fori(0, BPG) as i:
                    gather(i + (NG + g) * BPG, i * TB + g * TPG, g)


def kernel(L0_attn_x, L0_attn_Wq, L0_attn_bq, L0_attn_Wk, L0_attn_bk, L0_attn_Wv, L0_attn_bv, L0_attn_gamma,
           L0_attn_beta, L0_ffn_ln_gamma, L0_ffn_ln_beta, L0_ffn_router_w, L0_ffn_gate_up_w, L0_ffn_down_w,
           L0_ffn_shared_gate_up_w, L0_ffn_shared_down_w):
    import numpy as np
    import concourse.bacc as bacc
    from concourse.bass_utils import run_bass_kernel_spmd

    nc = bacc.Bacc("TRN2", target_bir_lowering=False, num_devices=1)
    given = dict(x=np.ascontiguousarray(L0_attn_x).reshape(NT, P, D), wq=L0_attn_Wq, bq=L0_attn_bq, wk=L0_attn_Wk,
                 bk=L0_attn_bk, wv=L0_attn_Wv, bv=L0_attn_bv, ga=L0_attn_gamma, ba=L0_attn_beta, gf=L0_ffn_ln_gamma,
                 bf=L0_ffn_ln_beta, rw=L0_ffn_router_w, guw=L0_ffn_gate_up_w, dnw=L0_ffn_down_w,
                 sguw=L0_ffn_shared_gate_up_w, sdnw=L0_ffn_shared_down_w)
    arrays = {f"in_{n}": np.ascontiguousarray(a) for n, a in given.items()}
    args = [nc.dram_tensor(n, a.shape, mybir.dt.from_np(a.dtype), kind="ExternalInput").ap() for n, a in arrays.items()]
    out = nc.dram_tensor("out", (NT, P, D), F32, kind="ExternalOutput").ap()
    xs = [nc.dram_tensor(f"rows{g}", (ROWS, D), F32).ap() for g in range(NG)]
    ys = [nc.dram_tensor(f"results{g}", (NBLK * P, D), F32).ap() for g in range(NG)]
    macaron(nc, *args, out, xs, ys)
    r = run_bass_kernel_spmd(nc, [arrays], core_ids=[0])
    return r.results[0]["out"].reshape(L0_attn_x.shape)
```

```python
from contextlib import ExitStack

import concourse.bass as bass
from concourse import mybir

F32 = mybir.dt.float32
BF16 = mybir.dt.bfloat16
I32 = mybir.dt.int32
ALU = mybir.AluOpType
ACT = mybir.ActivationFunctionType
AX_X = mybir.AxisListType.X

P = 128
D = 128
NT = 32
TB = 4
NG = 2
TPG = NT // NG
BPG = TPG // TB
NE = 8
FF = 384
FC = FF // P
REGION = TPG * P
MAXB = 2 * TPG + NE - 1
NBLK = -(-MAXB // 4) * 4
SPARE = NBLK - 2 * TPG
ROWS = NE * REGION + SPARE * P
EPS = 1e-5
SCALE = 128 ** -0.5
SLOPE = 0.01
TAKEN = -3.0e38
TAKEN_BELOW = -2.9e38
RSQRT_SEED = float(0x5F3759DF)
KTOP = 32
NSTEP = 3


def macaron(nc, x, wq, bq, wk, bk, wv, bv, ga, ba, gf, bf, rw, guw, dnw, sguw, sdnw, out, xs, ys):
    ctx = ExitStack()
    with ctx:
        def sb(name, shape, dt=F32):
            return ctx.enter_context(nc.sbuf_tensor(name, shape, dt))

        def sem(name):
            return ctx.enter_context(nc.semaphore(name))

        def bank(name):
            return ctx.enter_context(nc.psum_tensor(name, [P, TB, P], F32))

        ps_g, ps_u, ps_h = bank("ps_g"), bank("ps_u"), bank("ps_h")
        ps_x, ps_y = bank("ps_x"), bank("ps_y")
        w0, w1 = bank("w0"), bank("w1")
        ps_s = bank("ps_s")
        ps_lg = ps_s[:, 0, 0:TB * NE].rearrange("p (t e) -> p t e", e=NE)
        ps_pf = ps_s[:, 1, 0:(TB + 1) * NE].rearrange("p (t e) -> p t e", e=NE)

        def ff(t):
            return t[:, 0:FC, :].rearrange("p c f -> p (c f)")

        ident = sb("ident", [P, P])
        upper = sb("upper", [P, P], BF16)
        ones = sb("ones", [P, P], BF16)
        one_f = sb("one_f", [P, P])
        first_w = sb("first_w", [P, NE])
        region0 = sb("region0", [P, NE])
        full_at = sb("full_at", [P, TPG])
        blk_no = sb("blk_no", [P, NBLK])
        zeros = sb("zeros", [P, 2048])
        ga_b, ba_b, gf_b, bf_b, bv_b = (sb(n, [P, D]) for n in ("ga_b", "ba_b", "gf_b", "bf_b", "bv_b"))
        bq_c, bk_c = sb("bq_c", [P, 1]), sb("bk_c", [P, 1])

        raw_gu = sb("raw_gu", [P, NE, 2 * FC, D])
        raw_dn = sb("raw_dn", [P, NE, FF])
        raw_sm = sb("raw_sm", [P, 6, P])
        raw_rw = sb("raw_rw", [NE, D])
        gu_t = sb("gu_t", [P, NE, 2 * FF])
        dn_t = sb("dn_t", [P, NE, FF])
        sm_t = sb("sm_t", [P, 6, P])
        rw_t = sb("rw_t", [P, NE])
        sg_t, su_t, sd_t, wq_t, wk_t, wv_t = (sm_t[:, n, :] for n in range(6))

        xres = sb("xres", [P, NT, D])
        slots = sb("slots", [P, 2, NT], I32)
        lg_all = sb("lg_all", [P, NT, NE])
        oh_all = [sb(f"oh_all{c}", [P, NT, NE]) for c in range(2)]
        m1_all = sb("m1_all", [P, NT])
        gates = sb("gates", [P, 2, NT])
        run = sb("run", [P, NE])

        bn6 = sb("bn6", [P, NT, 6])
        mv0, nv0, ny0, nt0 = sb("mv0", [P, NT, 2]), sb("nv0", [P, NT]), sb("ny0", [P, NT]), sb("nt0", [P, NT])
        mva, nva, nya, nta = sb("mva", [P, 2 * TB, 2]), sb("nva", [P, 2 * TB]), sb("nya", [P, 2 * TB]), sb("nta", [P, 2 * TB])
        mvr, nvr, nyr, ntr = sb("mvr", [P, TB, 2]), sb("nvr", [P, TB]), sb("nyr", [P, TB]), sb("ntr", [P, TB])
        z_all = sb("z_all", [P, NT, D])
        z = sb("z", [P, TB, D])
        zg = sb("zg", [P, TB, D])
        nz = sb("nz", [P, TB, D])
        nz_t = sb("nz_t", [P, TB, P])
        sel = sb("sel", [P, 2 * TB + 1, NE], BF16)
        pos = sb("pos", [P, TB, NE])
        r8 = sb("r8", [P, TB, NE])
        r8b = sb("r8b", [P, TB, NE])
        f4 = sb("f4", [P, TB])
        s_idx = sb("s_idx", [P, 2, TB], I32)
        sg = sb("sg", [P, TB * P])
        sh = sb("sh", [P, TB, P])
        g_idx = [sb(f"g_idx{n}", [P, 2, TB], I32) for n in range(2)]
        yg = [sb(f"yg{n}", [P, TB, 2, D]) for n in range(2)]
        x1 = sb("x1", [P, TB, D])
        xn = sb("xn", [P, TB, D])
        xn_t = sb("xn_t", [P, TB, P])
        q_t = sb("q_t", [P, TB, P])
        k_t = sb("k_t", [P, TB, P])
        v = sb("v", [P, TB, D])
        sc = sb("sc", [P, TB, P])
        top = sb("top", [P, TB, KTOP])
        wk_s = sb("wk_s", [P, TB, P])
        nmax = sb("nmax", [P, TB])
        ex = sb("ex", [P, TB, P])
        pr = sb("pr", [P, TB, P])
        psum_p = sb("psum_p", [P, TB])
        rinv = sb("rinv", [P, TB])
        pr_t = sb("pr_t", [P, TB, P])
        o = sb("o", [P, TB, D])
        lr = sb("lr", [P, TB, D])
        rr = sb("rr", [P, TB, D])
        rn = sb("rn", [P, TB, D])
        rg = sb("rg", [P, TB, D])
        x1b = sb("x1b", [P, TB, D])
        fin = [sb(f"fin{n}", [P, TB, D]) for n in range(2)]

        gt = sb("gt", [P, TPG, NE])
        g4 = sb("g4", [P, 6, TPG])
        cnt = sb("cnt", [P, NE])
        nbk = sb("nbk", [P, NE])
        bend = sb("bend", [P, NE])
        shift = sb("shift", [P, NE])
        mv16 = sb("mv16", [P, TPG])
        cmp16 = sb("cmp16", [P, NE, TPG])
        cmpb = sb("cmpb", [P, NBLK, NE])
        cmpb2 = sb("cmpb2", [P, NBLK, NE])
        be = sb("be", [P, NBLK])
        bs = sb("bs", [P, NBLK])
        bt = sb("bt", [P, NBLK])
        tab_w = [sb(f"tab_w{n}", [P, NBLK], I32) for n in range(2 * NG)]
        tab_r = [sb(f"tab_r{n}", [P, NBLK], I32) for n in range(2 * NG)]

        xin = sb("xin", [P, 4, D])
        x_t = sb("x_t", [P, 2, P])
        sil = sb("sil", [P, 2, FF])
        h = sb("h", [P, 2, FF])
        h_t = sb("h_t", [P, 2, FF])
        yb = sb("yb", [P, 2, D])

        ld_c, ld_sm = sem("ld_c"), sem("ld_sm")
        ld_x = [sem(f"ld_x{g}") for g in range(NG)]
        ld_gu, ld_dn = sem("ld_gu"), sem("ld_dn")
        cst, pc, zfill, ready_z = sem("cst"), sem("pc"), sem("zfill"), sem("ready_z")
        wt_ps, wt_a, wt_v = sem("wt_ps"), sem("wt_a"), sem("wt_v")
        z0_bn, z0_ag, z0_nw, z0_done, zg0_done = (sem(n) for n in ("z0_bn", "z0_ag", "z0_nw", "z0_done", "zg0_done"))
        rt_bn, rt_ag, rt_nw, z_done, zg_done, nz_done = (sem(n) for n in ("rt_bn", "rt_ag", "rt_nw", "z_done", "zg_done", "nz_done"))
        nzT_ps, nzT_sb, lg_ps, lg_sb = (sem(n) for n in ("nzT_ps", "nzT_sb", "lg_ps", "lg_sb"))
        shG, shU, sg_done, shh, shD, xr_done = (sem(n) for n in ("shG", "shU", "sg_done", "shh", "shD", "xr_done"))
        rc, sel_done, pf_ps, scat, slot_cp = (sem(n) for n in ("rc", "sel_done", "pf_ps", "scat", "slot_cp"))
        tl, tl_e, bl, tab, gts, run0 = (sem(n) for n in ("tl", "tl_e", "bl", "tab", "gts", "run0"))
        gi, cb = sem("gi"), sem("cb")
        gath = [sem(f"gath{n}") for n in range(2)]
        at_bn, at_ag, at_nw, xn_done = (sem(n) for n in ("at_bn", "at_ag", "at_nw", "xn_done"))
        xnT_ps, xnT_sb, q_ps, q_sb, k_ps, k_sb, v_ps, v_sb = (sem(n) for n in ("xnT_ps", "xnT_sb", "q_ps", "q_sb", "k_ps", "k_sb", "v_ps", "v_sb"))
        s_ps, tk, nm_done, ex_done, pr_done, ri_done, prT_ps, prT_sb, o_ps, o_sb = (
            sem(n) for n in ("s_ps", "tk", "nm_done", "ex_done", "pr_done", "ri_done", "prT_ps", "prT_sb", "o_ps", "o_sb"))
        lr_done, rr_done, ob_bn, ob_ag, rn_done, rg_done, x1b_done, x2_done = (
            sem(n) for n in ("lr_done", "rr_done", "ob_bn", "ob_ag", "rn_done", "rg_done", "x1b_done", "x2_done"))
        sc_sb = sem("sc_sb")
        rrow = sem("rrow")
        passed = {e: sem(f"passed_{n}") for e, n in ((nc.vector.engine, "dve"), (nc.gpsimd.engine, "pool"))}
        out_st = [sem(f"out_st{n}") for n in range(2)]
        xin_ld = [sem(f"xin_ld{k}") for k in range(4)]
        yst = [sem(f"yst{k}") for k in range(2)]
        xT_ps, xT_sb, g_ps, u_ps, sil_done, h_done, hT_ps, hT_sb, y_ps, y_sb = (
            sem(n) for n in ("xT_ps", "xT_sb", "g_ps", "u_ps", "sil_done", "h_done", "hT_ps", "hT_sb", "y_ps", "y_sb"))

        CREDITS = [(xT_ps, 4), (xT_sb, 2), (u_ps, 2), (sil_done, 2), (h_done, 2), (hT_ps, 2), (hT_sb, 2), (y_ps, 2),
                   (y_sb, 2), (yst[0], 16), (yst[1], 16), (zg_done, 1), (shh, 1), (xr_done, 1), (shU, 1), (shD, 1),
                   (nzT_ps, 1), (slot_cp, 1), (o_sb, TB), (prT_sb, 1), (pr_done, TB),
                   (lr_done, 1), (x1b_done, 1), (x2_done, 1),
                   (out_st[0], 16), (out_st[1], 16)]

        ctx.enter_context(nc.allow_low_precision(reason="rows' numbers are whole and below 2**24, exact in float32"))
        block = ctx.enter_context(nc.Block())
        N_RT = 2 + 3 * NSTEP
        N_PICK = 11
        N_ROWS = 6
        N_RC = N_PICK + N_ROWS
        N_TOP = 2 * TB * (KTOP // 8)
        QB = NBLK // (BPG + 1)
        OUTS = [BPG + BPG // 2, BPG // 2]
        R2 = NG * BPG
        assert QB * (BPG + 1) == NBLK and QB % 4 == 0

        def apart(eng):
            eng.sem_inc(passed[eng.engine], 1)

        @block.sync
        def _(sp):
            for s, n in CREDITS:
                sp.sem_inc(s, n)
            for n in range(BPG * NG):
                sp.dma_start(xres[:, n * TB:(n + 1) * TB, :],
                             x[n * TB:(n + 1) * TB].rearrange("t p d -> p t d")).then_inc(ld_x[n // BPG], 16)
            sp.dma_start(raw_gu[:, 0:NE // 2], guw[0:NE // 2].rearrange("e (c p) d -> p e c d", p=P)).then_inc(ld_gu, 16)
            sp.dma_start(raw_gu[:, NE // 2:], guw[NE // 2:].rearrange("e (c p) d -> p e c d", p=P)).then_inc(ld_gu, 16)
            sp.dma_start(raw_dn[:], dnw.rearrange("e p f -> p e f")).then_inc(ld_dn, 16)

            def load(ph, g, b, m, k):
                row = sp.value_load(tab_r[ph][0:1, bass.ds(b, 1)], min_val=0, max_val=ROWS - P)
                sp.wait_ge(xT_ps, ph * NBLK + b + 1)
                sp.dma_start(xin[:, k, :], xs[g][bass.ds(row, P), :]).then_inc(xin_ld[k], 16)

            def store(ph, g, b, k):
                sp.wait_ge(y_sb, ph * NBLK + b + 3)
                sp.dma_start(ys[g][bass.ds(b * P, P), :], yb[:, k, :]).then_inc(yst[k], 16)

            def blocks(ph, g):
                sp.wait_ge(tab, ph + 1)
                sp.wait_ge(scat, 2 * TB * 16 * (ph + 1) * BPG)
                def slot(b, q):
                    if not isinstance(b, int) or b + 3 < NBLK:
                        load(ph, g, b + 3, None, (q + 3) % 4)
                    if not isinstance(b, int) or b >= 2:
                        store(ph, g, b - 2, q % 2)
                for b in range(3):
                    load(ph, g, b, None, b)
                for b in range(4):
                    slot(b, b)
                with sp.Fori(0, NBLK // 4 - 2) as i:
                    for q in range(4):
                        slot(i * 4 + (4 + q), q)
                for b in range(NBLK - 4, NBLK + 2):
                    slot(b, b % 4)

            for g in range(NG):
                blocks(g, g)
            for g in range(NG):
                blocks(NG + g, g)
            for n in range(2):
                sp.wait_ge(out_st[n], 16 * (1 + OUTS[n]))
            for k in range(2):
                sp.wait_ge(yst[k], 16 * (1 + 2 * NG * NBLK // 2))

        @block.tensor
        def _(pe):
            pe.wait_ge(cst, 1)
            pe.wait_ge(ld_sm, 16 * 6)
            for n in range(3):
                pe.transpose(w0[:, n, :], raw_sm[:, n, :], ident[:])
            for n in range(3):
                pe.transpose(w1[:, n, :], raw_sm[:, 3 + n, :], ident[:])
            pe.transpose(ps_lg[:, 0, :], raw_rw[:], ident[0:NE, 0:NE]).then_inc(wt_ps, 1)
            pe.wait_ge(ld_dn, 16)
            pe.wait_ge(ld_gu, 32)
            for e in range(NE):
                if e >= 1:
                    pe.wait_ge(wt_a, 2 * e + 1)
                if e >= 2:
                    pe.wait_ge(wt_v, e)
                for c in range(FC):
                    pe.transpose((ps_g, ps_x)[e % 2][:, c, :], raw_gu[:, e, c, :], ident[:])
                for c in range(FC):
                    pe.transpose((ps_u, ps_y)[e % 2][:, c, :], raw_gu[:, e, FC + c, :], ident[:])
                for c in range(FC):
                    t = pe.transpose(ps_h[:, c, :], raw_dn[:, e, c * P:(c + 1) * P], ident[:])
                t.then_inc(wt_ps, 1)
            pe.wait_ge(wt_a, 1 + 2 * NE)
            pe.wait_ge(wt_v, 1 + NE)

            def logits(R, a, after):
                pe.wait_ge(nz_done, R + 1)
                pe.wait_ge(shh, R + 1)
                if a is not None:
                    pe.wait_ge(v_sb, a + 1)
                if after is not None:
                    pe.wait_ge(prT_sb, after + 1)
                for k in range(TB):
                    t = pe.transpose(w1[:, k, :], nz[:, k, :], ident[:])
                t.then_inc(nzT_ps, 1)
                pe.wait_ge(nzT_sb, R + 1)
                pe.wait_ge(xr_done, R + 1)
                for k in range(TB):
                    t = pe.matmul(ps_lg[:, k, :], nz_t[:, k, :], rw_t[:], start=True, stop=True)
                t.then_inc(lg_ps, 1)

            def shared_up(R, a, after):
                if a is not None:
                    pe.wait_ge(sc_sb, a + 1)
                if after is not None:
                    pe.wait_ge(o_sb, TB * (after + 1))
                pe.matmul(w0[:], sg_t, nz_t[:], start=True, stop=True).then_inc(shG, 1)
                pe.matmul(w1[:], su_t, nz_t[:], start=True, stop=True).then_inc(shU, 1)

            def prefixes(R):
                pe.wait_ge(sel_done, R + 1)
                pe.matmul(ps_pf, upper[:], sel[:, TB:, :], start=True, stop=False)
                for n in range(1, TB + 1):
                    t = pe.matmul(ps_pf, ones[:], sel[:, TB - n:2 * TB + 1 - n, :], start=False, stop=(n == TB))
                t.then_inc(pf_ps, 1)

            def shared_down(R):
                pe.wait_ge(shh, R + 2)
                for k in range(TB):
                    t = pe.matmul(w0[:, k, :], sh[:, k, :], sd_t, start=True, stop=True)
                t.then_inc(shD, 1)

            def turn_x(a, done):
                pe.wait_ge(xn_done, TB * (a + 1))
                pe.wait_ge(o_sb, TB * (a + 1))
                pe.wait_ge(xr_done, done + 1)
                for k in range(TB):
                    t = pe.transpose(w0[:, k, :], xn[:, k, :], ident[:])
                t.then_inc(xnT_ps, 1)

            def queries_keys(a, done):
                pe.wait_ge(xnT_sb, a + 1)
                pe.wait_ge(prT_sb, a + 1)
                pe.wait_ge(shh, done + 1)
                pe.matmul(w1[:], wq_t, xn_t[:], start=True, stop=True).then_inc(q_ps, 1)
                pe.matmul(w0[:], wk_t, xn_t[:], start=True, stop=True).then_inc(k_ps, 1)

            def values(a):
                pe.wait_ge(q_sb, a + 1)
                for k in range(TB):
                    t = pe.matmul(w1[:, k, :], xn_t[:, k, :], wv_t, start=True, stop=True)
                t.then_inc(v_ps, 1)

            def scores(a):
                pe.wait_ge(k_sb, a + 1)
                for k in range(TB):
                    t = pe.matmul(w0[:, k, :], q_t[:, k, :], k_t[:, k, :], start=True, stop=True)
                t.then_inc(s_ps, 1)

            def turn_p(a, R):
                pe.wait_ge(pr_done, TB * (a + 2))
                pe.wait_ge(v_sb, a + 1)
                if R is not None:
                    pe.wait_ge(shh, R + 2)
                for k in range(TB):
                    t = pe.transpose(w1[:, k, :], pr[:, k, :], ident[:])
                t.then_inc(prT_ps, 1)

            def mix(a, R):
                pe.wait_ge(prT_sb, a + 2)
                if R is not None:
                    pe.wait_ge(xr_done, R + 2)
                for k in range(TB):
                    t = pe.matmul(w0[:, k, :], pr_t[:, k, :], v[:, k, :], start=True, stop=True)
                t.then_inc(o_ps, 1)

            def slot(ph, b, q):
                    static = isinstance(b, int)
                    B = b + ph * NBLK
                    k = q % 2
                    if not static or b + 1 < NBLK:
                        k4 = (q + 1) % 4
                        pe.wait_ge(xin_ld[k4], (B + (1 - k4 + 4)) * 4)
                        pe.wait_ge(xT_sb, B + 3)
                        pe.transpose(ps_x[:, 0, :], xin[:, k4, :], ident[:]).then_inc(xT_ps, 1)
                    if not static or b < NBLK:
                        off = pe.value_load(tab_w[ph][0:1, bass.ds(b, 1)], min_val=0, max_val=(NE - 1) * FF)
                        pe.wait_ge(xT_sb, B + 3)
                        pe.wait_ge(sil_done, B + 2)
                        gu = gu_t[:].rearrange("p e f -> p (e f)")
                        pe.matmul(ff(ps_g), x_t[:, k, :], gu[:, bass.ds(off * 2, FF)], start=True, stop=True).then_inc(g_ps, 1)
                        pe.wait_ge(h_done, B + 2)
                        pe.matmul(ff(ps_u), x_t[:, k, :], gu[:, bass.ds(off * 2 + FF, FF)], start=True, stop=True).then_inc(u_ps, 1)
                    if not static or 2 <= b:
                        off = pe.value_load(tab_w[ph][0:1, bass.ds(b - 2, 1)], min_val=0, max_val=(NE - 1) * FF)
                        pe.wait_ge(hT_sb, B + 1)
                        pe.wait_ge(y_sb, B)
                        dn = dn_t[:].rearrange("p e f -> p (e f)")
                        for c in range(FC):
                            t = pe.matmul(ps_y[:, 0, :], h_t[:, k, c * P:(c + 1) * P], dn[:, bass.ds(off + c * D, D)],
                                          start=(c == 0), stop=(c == FC - 1))
                        t.then_inc(y_ps, 1)
                    if not static or 1 <= b <= NBLK:
                        pe.wait_ge(h_done, B + 2)
                        pe.wait_ge(hT_sb, B + 1)
                        for c in range(FC):
                            t = pe.transpose(ps_h[:, c, :], h[:, 1 - k, c * P:(c + 1) * P], ident[:])
                        t.then_inc(hT_ps, 1)

            def first_x(ph):
                pe.wait_ge(tab, ph + 1)
                pe.wait_ge(xin_ld[0], (ph * (NBLK // 4) + 1) * 16)
                pe.wait_ge(xT_sb, ph * NBLK + 2)
                pe.transpose(ps_x[:, 0, :], xin[:, 0, :], ident[:]).then_inc(xT_ps, 1)

            def step(it, ph=None, a=None, R=None, done=None, after=None):
                def slots_(*qs):
                    if ph is not None:
                        for q in qs:
                            slot(ph, it * QB + q, q)
                slots_(0)
                if a is not None:
                    turn_x(a, done)
                slots_(1)
                if a is not None:
                    queries_keys(a, done)
                slots_(2)
                if a is not None:
                    values(a)
                slots_(3)
                if a is not None:
                    scores(a)
                if R is not None:
                    logits(R, a, after)
                slots_(4)
                if R is not None:
                    shared_up(R, a, after)
                slots_(5)
                if R is not None:
                    prefixes(R)
                    shared_down(R)
                slots_(6)
                if a is not None:
                    turn_p(a, R)
                slots_(7)
                if a is not None:
                    mix(a, R)

            def drain(ph):
                for b in (NBLK, NBLK + 1):
                    slot(ph, b, b % 4)

            step(0, R=0)
            with pe.Fori(1, BPG) as i:
                step(i, R=i)
            first_x(0)
            step(0, 0, R=BPG)
            with pe.Fori(1, BPG) as i:
                step(i, 0, R=i + BPG)
            step(BPG, 0)
            drain(0)
            for g in range(NG):
                a0, r0 = g * BPG, R2 + g * BPG
                first_x(1 + g)
                step(0, 1 + g, a=a0, done=r0)
                with pe.Fori(1, BPG - 1) as i:
                    step(i, 1 + g, a=i + a0, R=i + (r0 - 1), done=i + (r0 - 1))
                step(BPG - 1, 1 + g, a=a0 + BPG - 1, R=r0 + BPG - 2, done=r0 + BPG - 2)
                step(BPG, 1 + g, R=r0 + BPG - 1, after=a0 + BPG)
                drain(1 + g)
            first_x(3)
            step(0, 3)
            with pe.Fori(1, BPG) as i:
                step(i, 3)
            step(BPG, 3)
            drain(3)

        @block.scalar
        def _(act):
            act.dma_start(raw_sm[:, 0:2, :], sguw.rearrange("(c p) d -> p c d", p=P)).then_inc(ld_sm, 16)
            for n, w in enumerate((sdnw, wq, wk, wv)):
                act.dma_start(raw_sm[:, 2 + n, :], w).then_inc(ld_sm, 16)
            act.dma_start(raw_rw[:], rw).then_inc(ld_sm, 16)
            for t, w in ((ga_b, ga), (ba_b, ba), (gf_b, gf), (bf_b, bf), (bv_b, bv)):
                act.dma_start(t[:], w.partition_broadcast(P)).then_inc(ld_c, 16)
            for t, w in ((bq_c, bq), (bk_c, bk)):
                act.dma_start(t[:], w.rearrange("(p o) -> p o", o=1)).then_inc(ld_c, 16)
            act.wait_ge(ready_z, 1)
            for g in range(NG):
                for n in range(0, ROWS, 16 * P):
                    m = min(16 * P, ROWS - n) // P
                    act.dma_start(xs[g][n:n + m * P].rearrange("(p r) d -> p (r d)", p=P), zeros[:, 0:m * D]).then_inc(zfill, 16)

            act.wait_ge(wt_ps, 1)
            act.copy(sm_t[:, 0:3, :], w0[:, 0:3, :]).then_inc(wt_a, 1)
            for e in range(NE):
                act.wait_ge(wt_ps, 2 + e)
                act.copy(gu_t[:, e, 0:FF], ff((ps_g, ps_x)[e % 2])).then_inc(wt_a, 1)
                act.copy(dn_t[:, e, :], ff(ps_h)).then_inc(wt_a, 1)

            def logits(R, tile):
                act.wait_ge(nzT_ps, R + 2)
                act.wait_ge(shU, R + 1)
                act.copy(nz_t[:], w1[:]).then_inc(nzT_sb, 1)
                act.wait_ge(lg_ps, R + 1)
                act.copy(lg_all[:, bass.ds(tile, TB), :], ps_lg).then_inc(lg_sb, 1)

            def shared(R):
                act.wait_ge(shG, R + 1)
                act.wait_ge(shh, R + 1)
                act.activation(sg[:], w0[:].rearrange("p t d -> p (t d)"), ACT.Silu).then_inc(sg_done, 1)

            def tail(ph):
                act.wait_ge(tl, ph * 9 + 1)
                act.activation(gt[:], gt[:], ACT.Exp).then_inc(tl_e, 1)
                act.wait_ge(tl, ph * 9 + 7)
                act.activation(g4[:, 4, :], g4[:, 3, :], ACT.Exp).then_inc(tl_e, 1)

            def turn_x(a):
                act.wait_ge(xnT_ps, a + 1)
                act.copy(xn_t[:], w0[:]).then_inc(xnT_sb, 1)

            def queries_keys(a):
                act.wait_ge(q_ps, a + 1)
                act.activation(q_t[:], w1[:], ACT.Identity, bias=bq_c[:]).then_inc(q_sb, 1)
                act.wait_ge(k_ps, a + 1)
                act.activation(k_t[:], w0[:], ACT.Identity, bias=bk_c[:]).then_inc(k_sb, 1)

            def scores(a):
                act.wait_ge(s_ps, a + 1)
                act.wait_ge(pr_done, TB * (a + 1))
                act.copy(sc[:], w0[:]).then_inc(sc_sb, 1)

            def exps(a):
                act.wait_ge(nm_done, a + 1)
                for k in range(TB):
                    act.activation(ex[:, k, :], sc[:, k, :], ACT.Exp, bias=nmax[:, k:k + 1], scale=SCALE).then_inc(ex_done, 1)

            def turn_p(a):
                act.wait_ge(prT_ps, a + 1)
                act.copy(pr_t[:], w1[:]).then_inc(prT_sb, 1)

            def mix(a):
                act.wait_ge(o_ps, a + 1)
                act.wait_ge(ri_done, a + 1)
                act.wait_ge(lr_done, a + 1)
                for k in range(TB):
                    act.activation(o[:, k, :], w0[:, k, :], ACT.Copy, scale=rinv[:, k:k + 1]).then_inc(o_sb, 1)

            def first_x(ph):
                act.wait_ge(xT_ps, ph * NBLK + 5)
                act.wait_ge(u_ps, ph * NBLK + 1)
                act.copy(x_t[:, 0, :], ps_x[:, 0, :]).then_inc(xT_sb, 1)

            def slot(ph, b, q):
                static = isinstance(b, int)
                B = b + ph * NBLK
                k = q % 2
                if not static or b + 1 < NBLK:
                    act.wait_ge(xT_ps, B + 6)
                    act.wait_ge(u_ps, B + 2)
                    act.copy(x_t[:, 1 - k, :], ps_x[:, 0, :]).then_inc(xT_sb, 1)
                if not static or b < NBLK:
                    act.wait_ge(g_ps, B + 1)
                    act.wait_ge(h_done, B + 1)
                    act.activation(sil[:, k, :], ff(ps_g), ACT.Silu).then_inc(sil_done, 1)
                if not static or b >= 2:
                    act.wait_ge(y_ps, B + 1)
                    act.wait_ge(yst[k], (B - k) * 8)
                    act.copy(yb[:, k, :], ps_y[:, 0, :]).then_inc(y_sb, 1)
                if not static or 1 <= b <= NBLK:
                    act.wait_ge(hT_ps, B + 2)
                    act.wait_ge(y_ps, B)
                    act.copy(h_t[:, 1 - k, :], ff(ps_h)).then_inc(hT_sb, 1)

            def output(C, tile, n):
                act.wait_ge(cb, 2 * TB * (C + 1))
                act.dma_start(out[bass.ds(tile, TB)].rearrange("t p d -> p t d"), fin[n][:]).then_inc(out_st[n], 16)

            def step(it, ph=None, a=None, R=None, tile=None, C=None, ctile=None):
                def slots_(*qs):
                    if ph is not None:
                        for q in qs:
                            slot(ph, it * QB + q, q)
                slots_(0)
                if a is not None:
                    turn_x(a)
                slots_(1)
                if a is not None:
                    queries_keys(a)
                slots_(2, 3)
                if a is not None:
                    scores(a)
                if R is not None:
                    logits(R, tile)
                slots_(4)
                if a is not None:
                    exps(a)
                if R is not None:
                    shared(R)
                slots_(5, 6)
                if a is not None:
                    turn_p(a)
                slots_(7)
                if a is not None:
                    mix(a)
                if C is not None:
                    output(C, ctile, 0)

            def drain(ph):
                for b in (NBLK, NBLK + 1):
                    slot(ph, b, b % 4)

            step(0, R=0, tile=0)
            with act.Fori(1, BPG) as i:
                step(i, R=i, tile=i * TB)
            tail(0)
            first_x(0)
            step(0, 0, R=BPG, tile=TPG)
            with act.Fori(1, BPG) as i:
                step(i, 0, R=i + BPG, tile=i * TB + TPG)
            step(BPG, 0)
            drain(0)
            tail(1)
            for g in range(NG):
                a0, r0, t0 = g * BPG, R2 + g * BPG, g * TPG
                first_x(1 + g)
                step(0, 1 + g, a=a0)
                with act.Fori(1, BPG - 1) as i:
                    step(i, 1 + g, a=i + a0, R=i + (r0 - 1), tile=i * TB + (t0 - TB))
                step(BPG - 1, 1 + g, a=a0 + BPG - 1, R=r0 + BPG - 2, tile=t0 + (BPG - 2) * TB)
                step(BPG, 1 + g, R=r0 + BPG - 1, tile=t0 + (BPG - 1) * TB)
                drain(1 + g)
                tail(2 + g)
            first_x(3)
            step(0, 3, C=R2, ctile=0)
            with act.Fori(1, BPG) as i:
                step(i, 3, C=i + R2, ctile=i * TB)
            step(BPG, 3)
            drain(3)
            with act.Fori(0, BPG // 2) as i:
                for n in range(2):
                    output(i * 2 + (R2 + BPG + n), i * (2 * TB) + (TPG + n * TB), n)

        @block.vector
        def _(dve):
            dve.memset(zeros[:], 0.0).then_inc(ready_z, 1)
            dve.wait_ge(wt_ps, 1)
            dve.tensor_copy(sm_t[:, 3:6, :], w1[:, 0:3, :])
            dve.tensor_copy(rw_t[:], ps_lg[:, 0, :]).then_inc(wt_v, 1)
            dve.wait_ge(cst, 1)
            dve.wait_ge(ld_c, 16 * 7)

            def row(t):
                return t.rearrange("p t d -> p (t d)")

            def rsqrt(chain, at, mv, nv, ny, nt, mult, add):
                n = [0]

                def link(ins):
                    n[0] += 1
                    ins.then_inc(chain, 1)
                    dve.wait_ge(chain, at + n[0])
                link(dve.tensor_scalar(nv, mv[:, :, 1], mult, add, ALU.mult, ALU.add))
                link(dve.tensor_scalar(ny.bitcast(I32), nv.bitcast(I32), -0.5, RSQRT_SEED, ALU.mult, ALU.add))
                for _ in range(NSTEP):
                    link(dve.scalar_tensor_tensor(nt, ny, -0.5, ny, ALU.mult, ALU.mult))
                    link(dve.tensor_tensor(nt, nt, nv, ALU.mult))
                    link(dve.scalar_tensor_tensor(ny, nt, 1.5, ny, ALU.add, ALU.mult))
                assert n[0] == N_RT

            def stats(src, mv, bn, ag, at, n0):
                for k in range(TB):
                    dve.bn_stats(bn6[:, n0 + k, :], src(k)).then_inc(bn, 1)
                for k in range(TB):
                    dve.wait_ge(bn, at + k + 1)
                    apart(dve)
                    dve.bn_aggr(mv[:, k, :], bn6[:, n0 + k, :]).then_inc(ag, 1)

            def normed(dst, src, mv, ny, done):
                for k in range(TB):
                    dve.tensor_scalar(dst[:, k, :], src(k), mv[:, k, 0:1], ny[:, k:k + 1],
                                      ALU.subtract, ALU.mult).then_inc(done, 1)

            def first_norms(g):
                dve.wait_ge(ld_x[g], 16 * BPG)
                t0, t1 = g * TPG, (g + 1) * TPG
                for t in range(t0, t1):
                    dve.bn_stats(bn6[:, t, :], xres[:, t, :]).then_inc(z0_bn, 1)
                for t in range(t0, t1):
                    dve.wait_ge(z0_bn, t + 1)
                    dve.bn_aggr(mv0[:, t, :], bn6[:, t, :]).then_inc(z0_ag, 1)
                dve.wait_ge(z0_ag, t1)
                rsqrt(z0_nw, g * N_RT, mv0[:, t0:t1, :], nv0[:, t0:t1], ny0[:, t0:t1], nt0[:, t0:t1], 1.0 + EPS, EPS * EPS)
                for t in range(t0, t1):
                    dve.tensor_scalar(z_all[:, t, :], xres[:, t, :], mv0[:, t, 0:1], ny0[:, t:t + 1],
                                      ALU.subtract, ALU.mult).then_inc(z0_done, 1)

            def bc(t):
                return t.rearrange("p (t o) -> p t o", o=1).broadcast_to([P, TB, NE])

            def tokens(t):
                return t.rearrange("p (o e) -> p o e", o=1).broadcast_to([P, TB, NE])

            def route_norm(A, tile):
                dve.wait_ge(x2_done, A + 2)
                apart(dve)
                stats(lambda k: row(xres[:, bass.ds(tile + k, 1), :]), mvr, rt_bn, rt_ag, A * TB, 0)
                dve.wait_ge(rt_ag, A * TB + TB)
                rsqrt(rt_nw, A * N_RT, mvr[:], nvr[:], nyr[:], ntr[:], 1.0 + EPS, EPS * EPS)
                dve.wait_ge(zg_done, A + 1)
                normed(z, lambda k: row(xres[:, bass.ds(tile + k, 1), :]), mvr, nyr, z_done)

            def pick(n, R, tile):
                fw = tokens(first_w[:])
                lg = lg_all[:, bass.ds(tile, TB), :]
                m1 = m1_all[:, bass.ds(tile, TB)]
                oh1 = oh_all[0][:, bass.ds(tile, TB), :]
                oh2 = oh_all[1][:, bass.ds(tile, TB), :]
                if n:
                    dve.wait_ge(rc, R * N_RC + n)
                else:
                    dve.wait_ge(lg_sb, R + 1)
                if n == 0:
                    t = dve.tensor_reduce(m1, lg, AX_X, ALU.max)
                elif n == 1:
                    t = dve.tensor_tensor(r8[:], lg, bc(m1), ALU.is_equal)
                elif n == 2 or n == 8:
                    t = dve.tensor_tensor(r8[:], r8[:], fw, ALU.mult)
                elif n == 3 or n == 9:
                    t = dve.tensor_reduce(f4[:], r8[:], AX_X, ALU.max)
                elif n == 4:
                    t = dve.tensor_tensor(oh1, fw, bc(f4[:]), ALU.is_equal)
                elif n == 5:
                    t = dve.scalar_tensor_tensor(r8b[:], oh1, TAKEN, lg, ALU.mult, ALU.add)
                elif n == 6:
                    t = dve.tensor_reduce(f4[:], r8b[:], AX_X, ALU.max)
                elif n == 7:
                    t = dve.tensor_tensor(r8[:], r8b[:], bc(f4[:]), ALU.is_equal)
                elif n == 10:
                    t = dve.tensor_tensor(oh2, fw, bc(f4[:]), ALU.is_equal)
                if n < N_PICK:
                    t.then_inc(rc, 1)
                else:
                    dve.tensor_tensor(sel[:, TB:2 * TB, :], oh1, oh2, ALU.add).then_inc(sel_done, 1)

            def shared(R):
                dve.wait_ge(shU, R + 2)
                dve.wait_ge(sg_done, R + 1)
                dve.wait_ge(shD, R + 1)
                dve.tensor_tensor(sh[:].rearrange("p t d -> p (t d)"), sg[:], w1[:].rearrange("p t d -> p (t d)"),
                                  ALU.mult).then_inc(shh, 1)

            def rows(R, tile):
                n = [N_PICK]

                def link(ins):
                    n[0] += 1
                    ins.then_inc(rc, 1)
                    dve.wait_ge(rc, R * N_RC + n[0])
                oh1 = oh_all[0][:, bass.ds(tile, TB), :]
                oh2 = oh_all[1][:, bass.ds(tile, TB), :]
                dve.wait_ge(pf_ps, R + 1)
                link(dve.tensor_tensor(pos[:], ps_pf[:, 0:TB, :], tokens(run[:]), ALU.add))
                link(dve.tensor_tensor(run[:], run[:], ps_pf[:, TB, :], ALU.add))
                link(dve.tensor_tensor(r8[:], oh1, pos[:], ALU.mult))
                link(dve.tensor_tensor(r8b[:], oh2, pos[:], ALU.mult))
                dve.wait_ge(slot_cp, R + 1)
                if not isinstance(R, int) or R:
                    dve.wait_ge(scat, R * (2 * TB * 16))
                link(dve.tensor_reduce(s_idx[:, 0, :], r8[:], AX_X, ALU.add))
                link(dve.tensor_reduce(s_idx[:, 1, :], r8b[:], AX_X, ALU.add))
                assert n[0] == N_RC

            def shared_joins(R, tile):
                dve.wait_ge(shD, R + 2)
                xr = xres[:, bass.ds(tile, TB), :]
                dve.scalar_tensor_tensor(xr, w0[:], 0.5, xr, ALU.mult, ALU.add).then_inc(xr_done, 1)

            def tail(ph, g):
                n = [0]
                N = 9

                def link(ins):
                    n[0] += 1
                    ins.then_inc(tl, 1)
                    dve.wait_ge(tl, ph * N + n[0])
                t0, t1 = g * TPG, (g + 1) * TPG
                m1 = m1_all[:, t0:t1].rearrange("p (t o) -> p t o", o=1).broadcast_to([P, TPG, NE])
                link(dve.tensor_tensor(gt[:], lg_all[:, t0:t1, :], m1, ALU.subtract))
                dve.wait_ge(tl_e, 2 * ph + 1)
                link(dve.tensor_reduce(g4[:, 0, :], gt[:], AX_X, ALU.add))
                link(dve.tensor_tensor(gt[:], gt[:], oh_all[1][:, t0:t1, :], ALU.mult))
                link(dve.tensor_reduce(g4[:, 1, :], gt[:], AX_X, ALU.add))
                link(dve.reciprocal(g4[:, 2, :], g4[:, 0, :]))
                link(dve.tensor_scalar(g4[:, 1, :], g4[:, 1, :], 1.0, None, ALU.subtract))
                link(dve.tensor_tensor(g4[:, 3, :], g4[:, 1, :], g4[:, 2, :], ALU.mult))
                dve.wait_ge(tl_e, 2 * ph + 2)
                link(dve.tensor_scalar(g4[:, 5, :], g4[:, 4, :], 2.0, 2.0, ALU.mult, ALU.add))
                link(dve.reciprocal(gates[:, 0, t0:t1], g4[:, 5, :]))
                assert n[0] == N
                dve.tensor_tensor(gates[:, 1, t0:t1], gates[:, 0, t0:t1], g4[:, 4, :], ALU.mult).then_inc(gts, 1)

            def block_list(ph):
                n = [0]
                N = 14

                def link(ins):
                    n[0] += 1
                    ins.then_inc(bl, 1)
                    dve.wait_ge(bl, ph * N + n[0])
                bn = blk_no[:].rearrange("p (b o) -> p b o", o=1).broadcast_to([P, NBLK, NE])
                link(dve.tensor_tensor(cnt[:], run[:], region0[:], ALU.subtract))
                link(dve.tensor_tensor(cmp16[:], cnt[:].rearrange("p (e o) -> p e o", o=1).broadcast_to([P, NE, TPG]),
                                       full_at[:].rearrange("p (o t) -> p o t", o=1).broadcast_to([P, NE, TPG]), ALU.is_gt))
                link(dve.tensor_reduce(nbk[:], cmp16[:], AX_X, ALU.add))
                link(dve.tensor_tensor_scan(bend[:], one_f[:, 0:NE], nbk[:], 0.0, ALU.mult, ALU.add))
                link(dve.tensor_tensor(cmpb[:], bn, bend[:].rearrange("p (o e) -> p o e", o=1).broadcast_to([P, NBLK, NE]), ALU.is_ge))
                link(dve.tensor_reduce(be[:], cmpb[:], AX_X, ALU.add))
                link(dve.tensor_tensor(cmpb2[:], cmpb[:], nbk[:].rearrange("p (o e) -> p o e", o=1).broadcast_to([P, NBLK, NE]), ALU.mult))
                link(dve.tensor_reduce(bs[:], cmpb2[:], AX_X, ALU.add))
                link(dve.tensor_tensor(bt[:], blk_no[:], bs[:], ALU.subtract))
                link(dve.tensor_scalar(bt[:], bt[:], float(P), None, ALU.mult))
                link(dve.scalar_tensor_tensor(tab_r[ph][:], be[:], float(REGION), bt[:], ALU.mult, ALU.add))
                link(dve.tensor_scalar(be[:], be[:], float(NE - 1), None, ALU.min))
                link(dve.tensor_tensor(shift[:], bend[:], nbk[:], ALU.subtract))
                link(dve.scalar_tensor_tensor(shift[:], shift[:], float(P), region0[:], ALU.mult, ALU.subtract))
                assert n[0] == N
                dve.tensor_scalar(tab_w[ph][:], be[:], float(FF), None, ALU.mult).then_inc(tab, 1)

            def result_rows(ph, g):
                n = [0]

                def link(ins):
                    n[0] += 1
                    ins.then_inc(rrow, 1)
                    dve.wait_ge(rrow, ph * 6 + n[0])
                t0, t1 = g * TPG, (g + 1) * TPG
                dve.wait_ge(slot_cp, (ph + 1) * BPG + 1)
                for c in range(2):
                    link(dve.tensor_tensor(gt[:], oh_all[c][:, t0:t1, :], shift[:].rearrange("p (o e) -> p o e", o=1).broadcast_to([P, TPG, NE]), ALU.mult))
                    link(dve.tensor_reduce(mv16[:], gt[:], AX_X, ALU.add))
                    link(dve.tensor_tensor(slots[:, c, t0:t1], slots[:, c, t0:t1], mv16[:], ALU.add))

            def start_group(ph):
                dve.tensor_copy(run[:], region0[:]).then_inc(run0, 1)
                dve.wait_ge(run0, ph + 1)

            def combine(C, m, tile, dst, n):
                dve.wait_ge(gath[n], (m + 1) * (2 * TB * 16))
                for k in range(TB):
                    dve.scalar_tensor_tensor(dst[:, k, :], yg[n][:, k, 0, :], gates[:, 0, bass.ds(tile + k, 1)],
                                             row(xres[:, bass.ds(tile + k, 1), :]), ALU.mult, ALU.add).then_inc(cb, 1)
                for k in range(TB):
                    dve.wait_ge(cb, C * (2 * TB) + (k + 1))
                    dve.scalar_tensor_tensor(dst[:, k, :], yg[n][:, k, 1, :], gates[:, 1, bass.ds(tile + k, 1)], dst[:, k, :],
                                             ALU.mult, ALU.add).then_inc(cb, 1)

            def leaky(A):
                dve.wait_ge(o_sb, TB * (A + 2))
                dve.scalar_tensor_tensor(lr[:], o[:], SLOPE, o[:], ALU.mult, ALU.max).then_inc(lr_done, 1)

            def norms(J, a, A):
                lo, hi = 0 if a is not None else TB, 2 * TB if A is not None else TB
                if a is not None:
                    dve.wait_ge(cb, (a + 1) * (2 * TB))
                    apart(dve)
                    stats(lambda k: x1[:, k, :], mva[:, 0:TB, :], at_bn, at_ag, a * TB, 0)
                if A is not None:
                    dve.wait_ge(rr_done, A + 1)
                    apart(dve)
                    stats(lambda k: rr[:, k, :], mva[:, TB:, :], ob_bn, ob_ag, A * TB, TB)
                    dve.wait_ge(ob_ag, A * TB + TB)
                if a is not None:
                    dve.wait_ge(at_ag, a * TB + TB)
                rsqrt(at_nw, J * N_RT, mva[:, lo:hi, :], nva[:, lo:hi], nya[:, lo:hi], nta[:, lo:hi], 1.0, EPS)
                if A is not None:
                    normed(rn, lambda k: rr[:, k, :], mva[:, TB:, :], nya[:, TB:], rn_done)
                if a is not None:
                    normed(xn, lambda k: x1[:, k, :], mva[:, 0:TB, :], nya[:, 0:TB], xn_done)

            def values(a):
                dve.wait_ge(v_ps, a + 1)
                dve.tensor_tensor(v[:], w1[:], bv_b[:].rearrange("p (o d) -> p o d", o=1).broadcast_to([P, TB, D]),
                                  ALU.add).then_inc(v_sb, 1)

            def top8(r, a, R, tile):
                if r == 0:
                    dve.wait_ge(sc_sb, a + 1)
                    apart(dve)
                at = a * N_TOP + 2 * TB * r
                src = wk_s if r else sc
                for k in range(TB):
                    if r:
                        dve.wait_ge(tk, at - TB + k + 1)
                        apart(dve)
                    dve.max(top[:, k, 8 * r:8 * r + 8], src[:, k, :]).then_inc(tk, 1)
                    if r and R is not None and k % 2:
                        pick(4 * (r - 1) + k // 2, R, tile)
                for k in range(TB):
                    dve.wait_ge(tk, at + k + 1)
                    apart(dve)
                    dve.match_replace(wk_s[:, k, :], top[:, k, 8 * r:8 * r + 8], src[:, k, :], TAKEN).then_inc(tk, 1)
                    if r and R is not None and k % 2:
                        pick(4 * (r - 1) + 2 + k // 2, R, tile)
                if r == 0:
                    dve.tensor_scalar(nmax[:], top[:, :, 0], -SCALE, None, ALU.mult).then_inc(nm_done, 1)

            def probabilities(a):
                for k in range(TB):
                    dve.wait_ge(tk, (a + 1) * N_TOP - TB + k + 1)
                    dve.wait_ge(ex_done, a * TB + k + 1)
                    dve.scalar_tensor_tensor(pr[:, k, :], wk_s[:, k, :], TAKEN_BELOW, ex[:, k, :], ALU.is_lt, ALU.mult,
                                             accum_out=psum_p[:, k:k + 1]).then_inc(pr_done, 1)
                dve.wait_ge(pr_done, TB * (a + 2))
                dve.reciprocal(rinv[:], psum_p[:]).then_inc(ri_done, 1)

            def slot(ph, b, q):
                static = isinstance(b, int)
                B = b + ph * NBLK
                k = q % 2
                if not static or b < NBLK:
                    dve.wait_ge(u_ps, B + 3)
                    dve.wait_ge(sil_done, B + 3)
                    dve.wait_ge(hT_ps, B + 1)
                    dve.tensor_tensor(h[:, k, :], sil[:, k, :], ff(ps_u), ALU.mult).then_inc(h_done, 1)

            def step(it, ph=None, J=None, a=None, R=None, A=None, atile=None, tile=None):
                def slots_(*qs):
                    if ph is not None:
                        for q in qs:
                            slot(ph, it * QB + q, q)
                if A is not None:
                    leaky(A)
                if a is not None:
                    dve.wait_ge(x1b_done, a + 1)
                    combine(a, a, atile, x1, 0)
                if a is not None or A is not None:
                    norms(J, a, A)
                slots_(0, 1)
                if A is not None:
                    route_norm(A, tile)
                slots_(2)
                if a is not None:
                    values(a)
                slots_(3)
                if a is not None:
                    top8(0, a, None, None)
                slots_(4)
                if a is not None:
                    top8(1, a, R, tile)
                    top8(2, a, R, tile)
                elif R is not None:
                    for n in range(8):
                        pick(n, R, tile)
                if R is not None:
                    shared(R)
                slots_(5)
                if a is not None:
                    top8(3, a, R, tile)
                elif R is not None:
                    for n in range(8, N_PICK + 1):
                        pick(n, R, tile)
                if a is not None:
                    probabilities(a)
                slots_(6)
                if R is not None:
                    rows(R, tile)
                    shared_joins(R, tile)
                slots_(7)

            def output(it, C, m, tile):
                dve.wait_ge(out_st[0], (it + 1) * 16)
                combine(C, m, tile, fin[0], 0)

            def group_end(ph):
                block_list(ph)
                tail(ph, ph % NG)
                result_rows(ph, ph % NG)

            for g in range(NG):
                first_norms(g)
            for e in range(NE):
                dve.wait_ge(wt_ps, 2 + e)
                dve.tensor_copy(gu_t[:, e, FF:2 * FF], ff((ps_u, ps_y)[e % 2])).then_inc(wt_v, 1)
            start_group(0)
            step(0, R=0, tile=0)
            with dve.Fori(1, BPG) as i:
                step(i, R=i, tile=i * TB)
            group_end(0)
            start_group(1)
            step(0, 0, R=BPG, tile=TPG)
            with dve.Fori(1, BPG) as i:
                step(i, 0, R=i + BPG, tile=i * TB + TPG)
            step(BPG, 0)
            group_end(1)
            for g in range(NG):
                a0, r0, t0, j0 = g * BPG, R2 + g * BPG, g * TPG, g * (BPG + 1)
                dve.wait_ge(gts, g + 1)
                start_group(2 + g)
                step(0, 1 + g, J=j0, a=a0, atile=t0)
                with dve.Fori(1, BPG - 1) as i:
                    step(i, 1 + g, J=i + j0, a=i + a0, A=i + (a0 - 1), R=i + (r0 - 1), atile=i * TB + t0, tile=i * TB + (t0 - TB))
                n = BPG - 1
                step(n, 1 + g, J=j0 + n, a=a0 + n, A=a0 + n - 1, R=r0 + n - 1, atile=t0 + n * TB, tile=t0 + (n - 1) * TB)
                step(BPG, 1 + g, J=j0 + BPG, A=a0 + n, R=r0 + n, tile=t0 + n * TB)
                group_end(2 + g)
            dve.wait_ge(gts, NG + 1)
            output(0, R2, R2, 0)
            step(0, 3)
            with dve.Fori(1, BPG) as i:
                output(i, i + R2, i + R2, i * TB)
                step(i, 3)
            step(BPG, 3)
            dve.wait_ge(gts, NG + 2)
            with dve.Fori(0, BPG // 2) as i:
                for n in range(2):
                    dve.wait_ge(out_st[n], (i + (BPG * (1 - n) + 1)) * 16)
                    combine(i * 2 + (R2 + BPG + n), i + (R2 + BPG) * (1 - n), i * (2 * TB) + (TPG + n * TB), fin[n], n)

        @block.gpsimd
        def _(pool):
            pool.memset(sel[:], 0.0).then_inc(pc, 1)
            pool.memset(one_f[:], 1.0).then_inc(pc, 1)
            pool.memset(ones[:], 1.0).then_inc(pc, 1)
            pool.wait_ge(pc, 3)
            pool.affine_select(out=ident[:], in_=one_f[:], compare_op=ALU.is_equal, fill=0.0, base=0,
                               pattern=[[-1, P]], channel_multiplier=1)
            pool.affine_select(out=upper[:], in_=ones[:], compare_op=ALU.is_ge, fill=0.0, base=-1,
                               pattern=[[1, P]], channel_multiplier=-1)
            pool.iota(first_w[:], pattern=[[-1, NE]], base=NE, channel_multiplier=0, allow_small_or_imprecise_dtypes=True)
            pool.iota(region0[:], pattern=[[REGION, NE]], base=0, channel_multiplier=0, allow_small_or_imprecise_dtypes=True)
            pool.iota(full_at[:], pattern=[[P, TPG]], base=0, channel_multiplier=0, allow_small_or_imprecise_dtypes=True)
            pool.iota(blk_no[:], pattern=[[1, NBLK]], base=0, channel_multiplier=0,
                      allow_small_or_imprecise_dtypes=True).then_inc(pc, 1)
            pool.wait_ge(pc, 4)
            pool.nop().then_inc(cst, 1)
            pool.wait_ge(ld_c, 16 * 7)

            def wide(t):
                return t[:].rearrange("p (o d) -> p o d", o=1).broadcast_to([P, TB, D])

            def affine(R, A, tile):
                if A is not None:
                    pool.wait_ge(z_done, TB * (A + 1))
                    pool.tensor_tensor(zg[:], z[:], wide(gf_b), ALU.mult).then_inc(zg_done, 1)
                    pool.wait_ge(zg_done, A + 2)
                pool.wait_ge(nzT_ps, R + 1)
                if not isinstance(R, int) or R:
                    pool.wait_ge(scat, R * (2 * TB * 16))
                pool.tensor_tensor(nz[:], zg[:] if A is not None else z_all[:, bass.ds(tile, TB), :], wide(bf_b),
                                   ALU.add).then_inc(nz_done, 1)

            def scatter(R, tile, g):
                pool.wait_ge(rc, (R + 1) * N_RC)
                apart(pool)
                pool.tensor_copy(slots[:, :, bass.ds(tile, TB)], s_idx[:]).then_inc(slot_cp, 1)
                pool.wait_ge(nz_done, R + 1)
                apart(pool)
                for k in range(TB):
                    for c in range(2):
                        pool.indirect_dma_start(xs[g], bass.IndirectOffsetOnAxis(s_idx[:, c, k:k + 1], 0),
                                                nz[:, k, :], None).then_inc(scat, 16)

            def gather(C, prior, tile, g, n):
                if prior is not None:
                    pool.wait_ge(cb, prior * (2 * TB))
                    apart(pool)
                pool.tensor_copy(g_idx[n][:], slots[:, :, bass.ds(tile, TB)]).then_inc(gi, 1)
                pool.wait_ge(gi, C + 1)
                apart(pool)
                for k in range(TB):
                    for c in range(2):
                        pool.indirect_dma_start(yg[n][:, k, c, :], None, ys[g],
                                                bass.IndirectOffsetOnAxis(g_idx[n][:, c, k:k + 1], 0)).then_inc(gath[n], 16)

            def residual(A):
                pool.wait_ge(lr_done, A + 2)
                pool.tensor_tensor(rr[:], lr[:], xn[:], ALU.add).then_inc(rr_done, 1)

            def attended(A, tile):
                pool.wait_ge(rn_done, TB * (A + 1))
                pool.tensor_tensor(rg[:], rn[:], wide(ga_b), ALU.mult).then_inc(rg_done, 1)
                pool.wait_ge(rg_done, A + 1)
                pool.tensor_tensor(xres[:, bass.ds(tile, TB), :], rg[:], x1b[:], ALU.add).then_inc(x2_done, 1)

            def bias(a):
                pool.wait_ge(cb, (a + 1) * (2 * TB))
                pool.wait_ge(x2_done, a + 1)
                pool.tensor_tensor(x1b[:], x1[:], wide(ba_b), ALU.add).then_inc(x1b_done, 1)

            def step(g, a=None, atile=None, A=None, R=None, tile=None, following=None):
                if A is not None:
                    residual(A)
                    attended(A, tile)
                if a is not None:
                    bias(a)
                if R is not None:
                    affine(R, A, tile)
                if following is not None:
                    gather(following, following, atile + TB, g, 0)
                if R is not None:
                    scatter(R, tile, g)

            def stored(ph):
                pool.wait_ge(rrow, 6 * (ph + 1))
                for k in range(2):
                    pool.wait_ge(yst[k], 16 * (1 + (ph + 1) * NBLK // 2))

            for t in range(NT):
                pool.wait_ge(z0_done, t + 1)
            for n in range(NT // TB):
                z4 = z_all[:, n * TB:(n + 1) * TB, :]
                pool.tensor_tensor(z4, z4, wide(gf_b), ALU.mult).then_inc(zg0_done, 1)
            pool.wait_ge(zg0_done, NT // TB)
            pool.wait_ge(zfill, 16 * NG * (-(-ROWS // (16 * P))))
            for g in range(NG):
                step(g, R=g * BPG, tile=g * TPG)
                with pool.Fori(1, BPG) as i:
                    step(g, R=i + g * BPG, tile=i * TB + g * TPG)
            for g in range(NG):
                a0, r0, t0 = g * BPG, R2 + g * BPG, g * TPG
                stored(g)
                gather(a0, a0 if a0 else None, t0, g, 0)
                step(g, a=a0, atile=t0, following=a0 + 1)
                with pool.Fori(1, BPG - 1) as i:
                    step(g, a=i + a0, atile=i * TB + t0, A=i + (a0 - 1), R=i + (r0 - 1), tile=i * TB + (t0 - TB),
                         following=i + (a0 + 1))
                n = BPG - 1
                step(g, a=a0 + n, atile=t0 + n * TB, A=a0 + n - 1, R=r0 + n - 1, tile=t0 + (n - 1) * TB)
                step(g, A=a0 + n, R=r0 + n, tile=t0 + n * TB)
            stored(2)
            with pool.Fori(0, BPG) as i:
                gather(i + R2, i + R2, i * TB, 0, 0)
            stored(3)
            with pool.Fori(0, BPG // 2) as i:
                for n in range(2):
                    gather(i * 2 + (R2 + BPG + n), i * 2 + (R2 + BPG - 1 + n), i * (2 * TB) + (TPG + n * TB), 1, n)


def kernel(L0_attn_x, L0_attn_Wq, L0_attn_bq, L0_attn_Wk, L0_attn_bk, L0_attn_Wv, L0_attn_bv, L0_attn_gamma,
           L0_attn_beta, L0_ffn_ln_gamma, L0_ffn_ln_beta, L0_ffn_router_w, L0_ffn_gate_up_w, L0_ffn_down_w,
           L0_ffn_shared_gate_up_w, L0_ffn_shared_down_w):
    import numpy as np
    import concourse.bacc as bacc
    from concourse.bass_utils import run_bass_kernel_spmd

    nc = bacc.Bacc("TRN2", target_bir_lowering=False, num_devices=1)
    given = dict(x=np.ascontiguousarray(L0_attn_x).reshape(NT, P, D), wq=L0_attn_Wq, bq=L0_attn_bq, wk=L0_attn_Wk,
                 bk=L0_attn_bk, wv=L0_attn_Wv, bv=L0_attn_bv, ga=L0_attn_gamma, ba=L0_attn_beta, gf=L0_ffn_ln_gamma,
                 bf=L0_ffn_ln_beta, rw=L0_ffn_router_w, guw=L0_ffn_gate_up_w, dnw=L0_ffn_down_w,
                 sguw=L0_ffn_shared_gate_up_w, sdnw=L0_ffn_shared_down_w)
    arrays = {f"in_{n}": np.ascontiguousarray(a) for n, a in given.items()}
    args = [nc.dram_tensor(n, a.shape, mybir.dt.from_np(a.dtype), kind="ExternalInput").ap() for n, a in arrays.items()]
    out = nc.dram_tensor("out", (NT, P, D), F32, kind="ExternalOutput").ap()
    xs = [nc.dram_tensor(f"rows{g}", (ROWS, D), F32).ap() for g in range(NG)]
    ys = [nc.dram_tensor(f"results{g}", (NBLK * P, D), F32).ap() for g in range(NG)]
    macaron(nc, *args, out, xs, ys)
    r = run_bass_kernel_spmd(nc, [arrays], core_ids=[0])
    return r.results[0]["out"].reshape(L0_attn_x.shape)
```

```python
from contextlib import ExitStack

import concourse.bass as bass
from concourse import mybir

F32 = mybir.dt.float32
BF16 = mybir.dt.bfloat16
I32 = mybir.dt.int32
ALU = mybir.AluOpType
ACT = mybir.ActivationFunctionType
AX_X = mybir.AxisListType.X

P = 128
D = 128
NT = 32
TB = 4
NG = 2
TPG = NT // NG
BPG = TPG // TB
NE = 8
FF = 384
FC = FF // P
REGION = TPG * P + P
MAXB = 2 * TPG + NE - 1
NBLK = -(-MAXB // 4) * 4
SPARE = NBLK - 2 * TPG
GROUP_ROWS = NE * REGION + SPARE * P
XW = D + 1
RESULTS = 2 * NT * P
EPS = 1e-5
SCALE = 128 ** -0.5
SLOPE = 0.01
TAKEN = -3.0e38
TAKEN_BELOW = -2.9e38
RSQRT_SEED = float(0x5F3759DF)
KTOP = 32
NSTEP = 3
STEPS = BPG + 2
SHARES = ((10, 0, 1, 0, 0, 0), (1, 3, 2, 2, 0, 2), (4, 4, 0, 1, 2, 3), (3, 3, 1, 1, 1, 2),
          (1, 3, 1, 4, 2, 1), (3, 1, 1, 2, 1, 2), (3, 2, 1, 1, 2, 3))
HOOKS = ((0, 2, 4, 6, 7), (10, 12, 14), (15, 17, 18), (20, 21, 22), (29, 30, 31))
HOOKS_LATE = ((1, 4, 7), (10, 13, 14), (15, 16), (18, 20, 23, 25), (29, 30, 31))
HOOKS_LAST = ((1, 4, 7), (9, 10, 12), (13, 14, 17), (29, 30), (31,))
VALUES, ROUTE_ROWS, NEXT_ROWS, AFTER, AFTER_LATE, PICKS, SHARED, SHARED_LATE = 9, 11, 12, 13, 12, 19, 26, 31
ROUTED = ((4, 0, 3, 0, 1, 3), (4, 0, 2, 0, 1, 4), (3, 0, 2, 0, 1, 4))
assert sum(map(sum, SHARES)) == 2 * NBLK and len(SHARES) == 1 + STEPS


def macaron(nc, x, wq, bq, wk, bk, wv, bv, ga, ba, gf, bf, rw, guw, dnw, sguw, sdnw, out, xs, yt):
    ctx = ExitStack()
    with ctx:
        def sb(name, shape, dt=F32):
            return ctx.enter_context(nc.sbuf_tensor(name, shape, dt))

        def sem(name):
            return ctx.enter_context(nc.semaphore(name))

        def bank(name):
            return ctx.enter_context(nc.psum_tensor(name, [P, TB, P], F32))

        ps_g, ps_u, ps_h = bank("ps_g"), bank("ps_u"), bank("ps_h")
        ps_x, ps_y = bank("ps_x"), bank("ps_y")
        w0, w1 = bank("w0"), bank("w1")
        ps_s = bank("ps_s")
        ps_lg = ps_s[:, 0, 0:TB * NE].rearrange("p (t e) -> p t e", e=NE)
        ps_pf = ps_s[:, 1, 0:(TB + 1) * NE].rearrange("p (t e) -> p t e", e=NE)

        def ff(t):
            return t[:, 0:FC, :].rearrange("p c f -> p (c f)")

        ident = sb("ident", [P, P])
        upper = sb("upper", [P, P], BF16)
        ones = sb("ones", [P, P], BF16)
        one_f = sb("one_f", [P, P])
        first_w = sb("first_w", [P, NE])
        region0 = sb("region0", [P, NG, NE])
        full_at = sb("full_at", [P, TPG])
        blk_no = sb("blk_no", [P, NBLK])
        result_no = sb("result_no", [P, NT, 2], I32)
        pads = sb("pads", [P, NE + SPARE, XW])
        ga_b, ba_b, bv_b = (sb(n, [P, D]) for n in ("ga_b", "ba_b", "bv_b"))
        bq_c, bk_c, gf_c, bf_c = (sb(n, [P, 1]) for n in ("bq_c", "bk_c", "gf_c", "bf_c"))

        raw_gu = sb("raw_gu", [P, NE, 2 * FC, D])
        raw_dn = sb("raw_dn", [P, NE, FF])
        raw_sm = sb("raw_sm", [P, 6, P])
        raw_rw = sb("raw_rw", [NE, D])
        gu_t = sb("gu_t", [P, NE, 2 * FF])
        dn_t = sb("dn_t", [P, NE, FF])
        sm_t = sb("sm_t", [P, 6, P])
        rw_t = sb("rw_t", [P, NE])
        sg_t, su_t, sd_t, wq_t, wk_t, wv_t = (sm_t[:, n, :] for n in range(6))

        xres = sb("xres", [P, NT, D])
        lg_all = sb("lg_all", [P, NT, NE])
        oh_all = [sb(f"oh_all{c}", [P, NT, NE]) for c in range(2)]
        m1_all = sb("m1_all", [P, NT])
        gates = sb("gates", [P, 2, NT])
        run = sb("run", [P, NE])

        bn6 = sb("bn6", [P, NT, 6])
        mv = sb("mv", [P, NT, 2])
        var_e = sb("var_e", [P, NT])
        rstd = sb("rstd", [P, NT])
        nw_t = sb("nw_t", [P, NT])
        nmr = sb("nmr", [P, TB])
        zz = [sb(f"zz{n}", [P, TB, 2, XW]) for n in range(BPG)]
        nz_t = sb("nz_t", [P, TB, P])
        sel = sb("sel", [P, 2 * TB + 1, NE], BF16)
        pos = sb("pos", [P, TB, NE])
        r8 = sb("r8", [P, TB, NE])
        r8b = sb("r8b", [P, TB, NE])
        f4 = sb("f4", [P, TB])
        s_idx = [sb(f"s_idx{n}", [P, 2, TB], I32) for n in range(BPG)]
        sg = sb("sg", [P, TB * P])
        sh = sb("sh", [P, TB, P])
        yg = [sb(f"yg{n}", [P, TB, 2, D]) for n in range(2)]
        yg_last = [raw_gu[:].rearrange("p e c d -> p (e c d)")[:, n * TB * 2 * D:(n + 1) * TB * 2 * D]
                   .rearrange("p (t c d) -> p t c d", c=2, d=D) for n in range(BPG)]
        xn = [sb(f"xn{n}", [P, TB, D]) for n in range(BPG)]
        xn_t = sb("xn_t", [P, TB, P])
        q_t = sb("q_t", [P, TB, P])
        k_t = sb("k_t", [P, TB, P])
        v = sb("v", [P, TB, D])
        sc = sb("sc", [P, TB, P])
        top = sb("top", [P, TB, KTOP])
        wk_s = sb("wk_s", [P, TB, P])
        nmax = sb("nmax", [P, TB])
        ex = sb("ex", [P, TB, P])
        pr = sb("pr", [P, TB, P])
        psum_p = sb("psum_p", [P, TB])
        rinv = sb("rinv", [P, TB])
        pr_t = sb("pr_t", [P, TB, P])
        o = sb("o", [P, TB, D])
        lr = sb("lr", [P, TB, D])
        rr = sb("rr", [P, TB, D])
        rn = sb("rn", [P, TB, D])
        rg = sb("rg", [P, TB, D])

        gt = sb("gt", [P, NT, NE])
        g4 = sb("g4", [P, 6, NT])
        cnt = sb("cnt", [P, NE])
        nbk = sb("nbk", [P, NE])
        bend = sb("bend", [P, NE])
        cmp16 = sb("cmp16", [P, NE, TPG])
        cmpb = sb("cmpb", [P, NBLK, NE])
        cmpb2 = sb("cmpb2", [P, NBLK, NE])
        be = sb("be", [P, NBLK])
        bs = sb("bs", [P, NBLK])
        bt = sb("bt", [P, NBLK])
        tab_w = sb("tab_w", [P, 2 * NG * NBLK], I32)
        tab_r = sb("tab_r", [P, 2 * NG * NBLK], I32)
        ends = sb("ends", [P, 2 * NG * NE], I32)

        xin = sb("xin", [P, 4, XW])
        idx = sb("idx", [P, 4], I32)
        x_t = sb("x_t", [P, 2, P])
        sil = sb("sil", [P, 2, FF])
        h = sb("h", [P, 2, FF])
        h_t = sb("h_t", [P, 2, FF])
        yb = sb("yb", [P, 4, D])

        ld_c, ld_sm, ld_dn = (sem(n) for n in ("ld_c", "ld_sm", "ld_dn"))
        ld_gu = [sem(f"ld_gu{n}") for n in range(2)]
        ld_x = [sem(f"ld_x{n}") for n in range(BPG + 1)]
        cst, pc, pad_z = sem("cst"), sem("pc"), sem("pad_z")
        wt_ps, wt_a, wt_v = sem("wt_ps"), sem("wt_a"), sem("wt_v")
        bn1, ag1, bn2, ag2, bn3, ag3, nw, nw2 = (sem(n) for n in ("bn1", "ag1", "bn2", "ag2", "bn3", "ag3", "nw", "nw2"))
        z_done, ids = sem("z_done"), sem("ids")
        nzT_ps, nzT_sb, lg_ps, lg_sb = (sem(n) for n in ("nzT_ps", "nzT_sb", "lg_ps", "lg_sb"))
        shG, shU, sg_done, shh, shD, xr_done = (sem(n) for n in ("shG", "shU", "sg_done", "shh", "shD", "xr_done"))
        rc, sel_done, pf_ps = (sem(n) for n in ("rc", "sel_done", "pf_ps"))
        scat = [sem(f"scat{n}") for n in range(BPG)]
        tl, tl_e, bl, ended, tab, gts, run0, padded = (
            sem(n) for n in ("tl", "tl_e", "bl", "ended", "tab", "gts", "run0", "padded"))
        cb = sem("cb")
        yld = [sem(f"yld{n}") for n in range(2)]
        yld_last = [sem(f"yld_last{n}") for n in range(BPG)]
        xn_done, xnT_ps, xnT_sb, q_ps, q_sb, k_ps, k_sb, v_ps, v_sb = (
            sem(n) for n in ("xn_done", "xnT_ps", "xnT_sb", "q_ps", "q_sb", "k_ps", "k_sb", "v_ps", "v_sb"))
        s_ps, sc_sb, tk, nm_done, ex_done, pr_done, ri_done, prT_ps, prT_sb, o_ps = (
            sem(n) for n in ("s_ps", "sc_sb", "tk", "nm_done", "ex_done", "pr_done", "ri_done", "prT_ps", "prT_sb", "o_ps"))
        o_sb = sem("o_sb")
        lr_done, rr_done, rn_done, rg_done, x2_done = (sem(n) for n in ("lr_done", "rr_done", "rn_done", "rg_done", "x2_done"))
        out_st = sem("out_st")
        passed = {e: sem(f"passed_{n}") for e, n in (
            (nc.vector.engine, "dve"), (nc.gpsimd.engine, "pool"), (nc.sync.engine, "sp"))}
        xin_ld = [sem(f"xin_ld{k}") for k in range(4)]
        yst = [sem(f"yst{k}") for k in range(4)]
        xT_ps, xT_sb, g_ps, u_ps, sil_done, h_done, hT_ps, hT_sb, y_ps, y_sb, idx_cp = (
            sem(n) for n in ("xT_ps", "xT_sb", "g_ps", "u_ps", "sil_done", "h_done", "hT_ps", "hT_sb", "y_ps", "y_sb", "idx_cp"))

        CREDITS = [(xT_ps, 4), (idx_cp, 4), (xT_sb, 2), (u_ps, 2), (sil_done, 2), (h_done, 2), (hT_ps, 2), (hT_sb, 2),
                   (y_ps, 2), (y_sb, 2), (shh, 1), (xr_done, 1), (prT_sb, 1), (pr_done, TB),
                   (lr_done, 1), (nm_done, 1), (o_ps, 1), (o_sb, 1), (v_sb, 1), (x2_done, 1), (rn_done, TB), (cb, 2 * 2 * TB)]

        ctx.enter_context(nc.allow_low_precision(reason="rows' numbers are whole and below 2**24, exact in float32"))
        block = ctx.enter_context(nc.Block())
        N_NW = 3 + 3 * NSTEP
        FIRST_NORMS = 3
        ROUTE_AT, AFTER_AT = TB, 2 * TB
        N_PICK = 11
        N_ROWS = 6
        N_RC = N_PICK + N_ROWS
        N_TOP = 2 * TB * (KTOP // 8)
        N_SCAT = 2 * TB * 16
        N_CB = 2 * TB
        R2 = NG * BPG

        def apart(eng):
            eng.sem_inc(passed[eng.engine], 1)

        ALONE = [()] * 6

        def halves(bs):
            return [(b, n) for b in bs for n in range(2)]

        def share(counts, step):
            first, parts = sum(map(sum, counts[:step])), []
            for n in counts[step]:
                parts.append(halves(range(NBLK))[first:first + n])
                first += n
            return parts

        AFTER_ROUTED = sum(map(sum, ROUTED)) // 16
        LOOP = halves(range(8))
        LAST = halves(range(NBLK - 4, NBLK + 2))
        LAST8 = halves(range(NBLK - 8, NBLK))
        DRAIN = halves(range(NBLK, NBLK + 2))
        FIRST = halves(range(4))

        def stages(s):
            return tuple(s - n if 0 <= s - n < BPG else None for n in range(3))

        def ahead(s):
            return s + 1 if s + 1 < BPG else None

        @block.sync
        def _(sp):
            for s, n in CREDITS:
                sp.sem_inc(s, n)

            def tokens(lo, hi, s):
                sp.dma_start(xres[:, lo:hi, :], x[lo:hi].rearrange("t p d -> p t d")).then_inc(s, 16)
            for n in range(BPG):
                tokens(n * TB, (n + 1) * TB, ld_x[n])
            sp.wait_ge(ld_c, 16 * 7)
            half = NE // 2
            sp.dma_start(raw_gu[:, 0:half], guw[0:half].rearrange("e (c p) d -> p e c d", p=P)).then_inc(ld_gu[0], 16)
            sp.dma_start(raw_dn[:], dnw.rearrange("e p f -> p e f")).then_inc(ld_dn, 16)
            sp.dma_start(raw_gu[:, half:], guw[half:].rearrange("e (c p) d -> p e c d", p=P)).then_inc(ld_gu[1], 16)
            tokens(TPG, NT, ld_x[BPG])

            def load(B, k):
                row = sp.value_load(tab_r[0:1, bass.ds(B, 1)], min_val=0, max_val=NG * GROUP_ROWS - P)
                sp.wait_ge(idx_cp, B + 1)
                sp.dma_start(xin[:, k, :], xs[bass.ds(row, P), :]).then_inc(xin_ld[k], 16)

            def fill(ph, e, n):
                row = sp.value_load(ends[0:1, bass.ds(e + ph * NE, 1)], min_val=0, max_val=NG * GROUP_ROWS - P)
                sp.dma_start(xs[bass.ds(row, P), :], pads[:, n, :]).then_inc(padded, 16)

            def fill_all(ph):
                sp.wait_ge(ended, ph + 1)
                apart(sp)
                for e in range(NE):
                    fill(ph, e, e)

            def begin(ph):
                sp.wait_ge(tab, ph + 1)
                apart(sp)
                sp.wait_ge(padded, (ph + 1) * (16 * NE))
                apart(sp)
                for n in range(BPG):
                    sp.wait_ge(scat[n], (ph + 1) * N_SCAT)
                    apart(sp)
                for b in range(3):
                    load(ph * NBLK + b, b)

            def stored(phases):
                for k in range(4):
                    sp.wait_ge(yst[k], phases * (16 * NBLK // 4) + 16)
                    apart(sp)

            def results_of(tile):
                return yt.rearrange("(t p c) d -> t p c d", p=P, c=2)[bass.ds(tile, TB)].rearrange("t p c d -> p t c d")

            def results(C, n, tile, phases):
                stored(phases)
                sp.wait_ge(cb, C * N_CB + N_CB)
                apart(sp)
                sp.dma_start(yg[n][:], results_of(tile)).then_inc(yld[n], 16)

            for k in range(4):
                sp.wait_ge(yst[k], 16)
            fill_all(0)
            begin(0)
            with sp.Fori(0, (NBLK - 4) // 4 - NE // 2) as i:
                for q in range(4):
                    load(i * 4 + (3 + q), (3 + q) % 4)
            sp.wait_ge(ended, 2)
            with sp.Fori(0, NE // 2) as i:
                for q in range(4):
                    load(i * 4 + (NBLK - 4 - 2 * NE + 3 + q), (3 + q) % 4)
                for n in range(2):
                    fill(1, i * 2 + n, n)
            load(NBLK - 1, 3)
            with sp.Fori(0, NG) as g:
                begin(g + 1)
                first = g * NBLK + NBLK
                for b in range(NBLK - 3):
                    load(first + (b + 3), (b + 3) % 4)
                    for n, at in enumerate((0, 1, 8, 10)):
                        if b == at:
                            results(g * BPG + n, n % 2, g * TPG + n * TB, g + 1)
                fill_all(g + 2)
            begin(3)
            with sp.Fori(0, BPG // 2) as i:
                for n in range(2):
                    for q in range(8):
                        load(i * 16 + (3 * NBLK + 8 * n + q + 3), (q + 3) % 4)
                        if q == 0:
                            results(i * 2 + (R2 + n), n, i * (2 * TB) + n * TB, 3)
            for b in range(BPG * 8 + 3, NBLK):
                load(3 * NBLK + b, b % 4)
            stored(4)
            for n in range(BPG):
                sp.dma_start(yg_last[n], results_of(TPG + n * TB)).then_inc(yld_last[n], 16)
            sp.wait_ge(out_st, 16 * R2)
            for k in range(4):
                sp.wait_ge(yst[k], 16 * (1 + NG * NBLK // 2))

        @block.tensor
        def _(pe):
            pe.wait_ge(cst, 1)
            pe.wait_ge(ld_sm, 16 * 6)
            for n in range(3):
                pe.transpose(w0[:, n, :], raw_sm[:, n, :], ident[:])
            for n in range(3):
                pe.transpose(w1[:, n, :], raw_sm[:, 3 + n, :], ident[:])
            pe.transpose(ps_lg[:, 0, :], raw_rw[:], ident[0:NE, 0:NE]).then_inc(wt_ps, 1)
            pe.wait_ge(wt_a, 1)
            pe.wait_ge(wt_v, 1)

            def expert(e):
                pe.wait_ge(ld_dn, 16)
                pe.wait_ge(ld_gu[e // (NE // 2)], 16)
                if e >= 1:
                    pe.wait_ge(wt_a, 2 * e + 1)
                if e >= 2:
                    pe.wait_ge(wt_v, e)
                for c in range(FC):
                    pe.transpose((ps_g, ps_x)[e % 2][:, c, :], raw_gu[:, e, c, :], ident[:])
                for c in range(FC):
                    pe.transpose((ps_u, ps_y)[e % 2][:, c, :], raw_gu[:, e, FC + c, :], ident[:])
                for c in range(FC):
                    t = pe.transpose(ps_h[:, c, :], raw_dn[:, e, c * P:(c + 1) * P], ident[:])
                t.then_inc(wt_ps, 1)

            def turn_p(A, done, keyed):
                pe.wait_ge(pr_done, (A + 2) * TB)
                pe.wait_ge(k_sb, keyed)
                pe.wait_ge(shh, done + 1)
                for k in range(TB):
                    t = pe.transpose(w1[:, k, :], pr[:, k, :], ident[:])
                t.then_inc(prT_ps, 1)

            def mix(A):
                pe.wait_ge(prT_sb, A + 2)
                pe.wait_ge(v_sb, A + 2)
                for k in range(TB):
                    t = pe.matmul(w1[:, k, :], pr_t[:, k, :], v[:, k, :], start=True, stop=True)
                t.then_inc(o_ps, 1)

            def turn_x(n, scored, done):
                pe.wait_ge(xn_done, (scored + 1) * TB)
                if n:
                    pe.wait_ge(sc_sb, scored)
                else:
                    pe.wait_ge(xr_done, done + 1)
                for k in range(TB):
                    t = pe.transpose(w0[:, k, :], xn[n][:, k, :], ident[:])
                t.then_inc(xnT_ps, 1)

            def turn_z(R, n, turned, valued):
                pe.wait_ge(z_done, (R + 1) * TB)
                pe.wait_ge(o_sb, turned + 1)
                pe.wait_ge(v_sb, valued + 1)
                pe.wait_ge(shh, R + 1)
                for k in range(TB):
                    t = pe.transpose(w1[:, k, :], zz[n][:, k, 0, 0:D], ident[:])
                t.then_inc(nzT_ps, 1)

            def queries(p):
                pe.wait_ge(xnT_sb, p + 1)
                pe.matmul(w0[:], wq_t, xn_t[:], start=True, stop=True).then_inc(q_ps, 1)

            def keys(p, R, done):
                pe.wait_ge(v_sb, p + 1)
                pe.wait_ge(shh, done + 1)
                if R is not None:
                    pe.wait_ge(nzT_sb, R + 1)
                pe.matmul(w1[:], wk_t, xn_t[:], start=True, stop=True).then_inc(k_ps, 1)

            def logits(R, joined=True):
                pe.wait_ge(nzT_sb, R + 1)
                if joined:
                    pe.wait_ge(xr_done, R + 1)
                for k in range(TB):
                    t = pe.matmul(ps_lg[:, k, :], nz_t[:, k, :], rw_t[:], start=True, stop=True)
                t.then_inc(lg_ps, 1)

            def values(a):
                pe.wait_ge(k_sb, a + 1)
                pe.wait_ge(o_sb, a + 1)
                for k in range(TB):
                    t = pe.matmul(w1[:, k, :], xn_t[:, k, :], wv_t, start=True, stop=True)
                t.then_inc(v_ps, 1)

            def scores(a, done):
                pe.wait_ge(q_sb, a + 1)
                pe.wait_ge(k_sb, a + 1)
                pe.wait_ge(xr_done, done + 1)
                for k in range(TB):
                    t = pe.matmul(w0[:, k, :], q_t[:, k, :], k_t[:, k, :], start=True, stop=True)
                t.then_inc(s_ps, 1)

            def shared_up(R, a, p):
                if a is not None:
                    pe.wait_ge(sc_sb, a + 1)
                    pe.wait_ge(v_sb, a + 2)
                if p is not None:
                    pe.wait_ge(q_sb, p + 1)
                    pe.wait_ge(k_sb, p + 1)
                pe.wait_ge(xr_done, R + 1)
                pe.matmul(w0[:], sg_t, nz_t[:], start=True, stop=True).then_inc(shG, 1)
                pe.matmul(w1[:], su_t, nz_t[:], start=True, stop=True).then_inc(shU, 1)

            def prefixes(R):
                pe.wait_ge(sel_done, R + 1)
                pe.matmul(ps_pf, upper[:], sel[:, TB:, :], start=True, stop=False)
                for n in range(1, TB + 1):
                    t = pe.matmul(ps_pf, ones[:], sel[:, TB - n:2 * TB + 1 - n, :], start=False, stop=(n == TB))
                t.then_inc(pf_ps, 1)

            def shared_down(R):
                pe.wait_ge(shh, R + 2)
                for k in range(TB):
                    t = pe.matmul(w0[:, k, :], sh[:, k, :], sd_t, start=True, stop=True)
                t.then_inc(shD, 1)

            held = {}

            def weights(B):
                return pe.value_load(tab_w[0:1, bass.ds(B, 1)], min_val=0, max_val=(NE - 1) * FF)

            def slot(B, b, half, x=True, up=True, down=True, turn=True, following=True, looped=False):
                k4, k = b % 4, b % 2
                if half == 0 and up:
                    if b not in held:
                        held[b] = weights(B)
                    off = held[b]
                    pe.wait_ge(xT_sb, B + 3)
                    pe.wait_ge(sil_done, B + 2)
                    gu = gu_t[:].rearrange("p e f -> p (e f)")
                    pe.matmul(ff(ps_g), x_t[:, k, :], gu[:, bass.ds(off * 2, FF)], start=True, stop=True).then_inc(g_ps, 1)
                    pe.wait_ge(h_done, B + 2)
                    pe.matmul(ff(ps_u), x_t[:, k, :], gu[:, bass.ds(off * 2 + FF, FF)], start=True, stop=True).then_inc(u_ps, 1)
                    for n in (b - 2, b - 1):
                        if n not in held and (looped or n >= 0):
                            held[n] = weights(B + (n - b))
                if half == 1 and x:
                    n4 = (k4 + 1) % 4
                    pe.wait_ge(xin_ld[n4], (B + (1 - n4)) * 4 + 16)
                    pe.wait_ge(xT_sb, B + 3)
                    pe.transpose(ps_x[:, 0, :], xin[:, n4, 0:D], ident[:]).then_inc(xT_ps, 1)
                if half == 1 and x and following:
                    held[b + 1] = weights(B + 1)
                if half == 1 and down:
                    off = held.pop(b - 2)
                    pe.wait_ge(hT_sb, B + 1)
                    pe.wait_ge(y_sb, B)
                    dn = dn_t[:].rearrange("p e f -> p (e f)")
                    for c in range(FC):
                        t = pe.matmul(ps_y[:, 0, :], h_t[:, k, c * P:(c + 1) * P], dn[:, bass.ds(off + c * D, D)],
                                      start=(c == 0), stop=(c == FC - 1))
                    t.then_inc(y_ps, 1)
                if half == 1 and turn:
                    pe.wait_ge(h_done, B + 2)
                    pe.wait_ge(hT_sb, B + 1)
                    for c in range(FC):
                        t = pe.transpose(ps_h[:, c, :], h[:, 1 - k, c * P:(c + 1) * P], ident[:])
                    t.then_inc(hT_ps, 1)

            def slots(first, hs):
                for b, half in hs:
                    slot(first + b, b, half, x=b + 1 < NBLK, up=b < NBLK, down=b >= 2, turn=1 <= b <= NBLK,
                         following=b + 1 < NBLK)

            def loop(B):
                held.clear()
                for b, half in LOOP:
                    slot(B + b, b, half, following=b < LOOP[-1][0], looped=True)
                held.clear()

            def first_x(first):
                pe.wait_ge(xin_ld[0], first * 4 + 16)
                pe.wait_ge(xT_sb, first + 2)
                pe.transpose(ps_x[:, 0, :], xin[:, 0, 0:D], ident[:]).then_inc(xT_ps, 1)

            def route(R, n, parts):
                slots(0, parts[0])
                turn_z(R, n, 0, 0)
                logits(R)
                slots(0, parts[2])
                shared_up(R, None, None)
                slots(0, parts[4])
                prefixes(R)
                shared_down(R)
                slots(0, parts[5])

            turn_z(0, 0, 0, 0)
            logits(0)
            for R in range(BPG):
                prefixes(R)
                shared_up(R, None, None)
                if R + 1 < BPG:
                    turn_z(R + 1, R + 1, 0, 0)
                expert(2 * R)
                if R + 1 < BPG:
                    logits(R + 1, joined=False)
                shared_down(R)
                expert(2 * R + 1)
            route(BPG, 0, ALONE)
            pe.wait_ge(wt_a, 1 + 2 * NE)
            pe.wait_ge(wt_v, 1 + NE)
            first_x(0)
            for n in range(1, BPG):
                route(BPG + n, n, share(ROUTED, n - 1))
            with pe.Fori(AFTER_ROUTED, NBLK // 8 - 1) as i:
                loop(i * 8)
            slots(0, LAST8)
            first_x(NBLK)
            slots(0, DRAIN)
            with pe.Fori(0, NG) as g:
                first = g * NBLK + NBLK
                held.clear()
                before = share(SHARES, 0)
                slots(first, before[0])
                turn_x(0, g * BPG, g * BPG + R2)
                slots(first, before[1])
                queries(g * BPG)
                keys(g * BPG, None, g * BPG + R2)
                slots(first, before[2])
                for s in range(STEPS):
                    parts, (a, A, Rn), p = share(SHARES, s + 1), stages(s), ahead(s)
                    done, turned, valued, keyed = (g * BPG + n for n in (
                        R2 + max(0, s - 2), min(s, BPG), min(s + 1, BPG), min(s + 1, BPG)))
                    a, A, p = (None if n is None else g * BPG + n for n in (a, A, p))
                    R = None if Rn is None else g * BPG + (R2 + Rn)
                    if a is not None:
                        scores(a, done)
                    if A is not None:
                        turn_p(A, done, keyed)
                    slots(first, parts[0])
                    if A is not None:
                        mix(A)
                    if a is not None:
                        values(a)
                    slots(first, parts[1])
                    if R is not None:
                        turn_z(R, Rn, turned, valued)
                    if p is not None:
                        turn_x(s + 1, p, done)
                    slots(first, parts[2])
                    if R is not None:
                        logits(R)
                    if p is not None:
                        queries(p)
                        keys(p, R, done)
                    slots(first, parts[3])
                    if R is not None:
                        shared_up(R, a, p)
                    slots(first, parts[4])
                    if R is not None:
                        prefixes(R)
                        shared_down(R)
                    slots(first, parts[5])
                slots(first, DRAIN)
                first_x(first + NBLK)
            slots(3 * NBLK, FIRST)
            with pe.Fori(0, NBLK // 8 - 1) as i:
                loop(i * 8 + (3 * NBLK + 4))
            slots(3 * NBLK, LAST)

        @block.scalar
        def _(act):
            act.dma_start(raw_sm[:, 0:2, :], sguw.rearrange("(c p) d -> p c d", p=P)).then_inc(ld_sm, 16)
            for n, w in enumerate((sdnw, wq, wk, wv)):
                act.dma_start(raw_sm[:, 2 + n, :], w).then_inc(ld_sm, 16)
            act.dma_start(raw_rw[:], rw).then_inc(ld_sm, 16)
            for t, w in ((gf_c, gf), (bf_c, bf), (bq_c, bq), (bk_c, bk)):
                act.dma_start(t[:], w.rearrange("(p o) -> p o", o=1)).then_inc(ld_c, 16)
            for t, w in ((ga_b, ga), (ba_b, ba), (bv_b, bv)):
                act.dma_start(t[:], w.partition_broadcast(P)).then_inc(ld_c, 16)
            act.wait_ge(wt_ps, 1)
            act.copy(sm_t[:, 0:3, :], w0[:, 0:3, :]).then_inc(wt_a, 1)
            act.wait_ge(ld_c, 16 * 7)

            def expert(e):
                act.wait_ge(wt_ps, 2 + e)
                act.copy(gu_t[:, e, 0:FF], ff((ps_g, ps_x)[e % 2])).then_inc(wt_a, 1)
                act.copy(dn_t[:, e, :], ff(ps_h)).then_inc(wt_a, 1)

            def turn_p(A):
                act.wait_ge(prT_ps, A + 1)
                act.copy(pr_t[:], w1[:]).then_inc(prT_sb, 1)

            def mix(A):
                act.wait_ge(o_ps, A + 2)
                act.wait_ge(lr_done, A + 1)
                act.copy(o[:], w1[:]).then_inc(o_sb, 1)

            def turn_x(a):
                act.wait_ge(xnT_ps, a + 1)
                act.copy(xn_t[:], w0[:]).then_inc(xnT_sb, 1)

            def turn_z(R):
                act.wait_ge(nzT_ps, R + 1)
                act.activation(nz_t[:], w1[:], ACT.Identity, bias=bf_c[:], scale=gf_c[:]).then_inc(nzT_sb, 1)

            def queries(a):
                act.wait_ge(q_ps, a + 1)
                act.activation(q_t[:], w0[:], ACT.Identity, bias=bq_c[:]).then_inc(q_sb, 1)

            def keys(a):
                act.wait_ge(k_ps, a + 1)
                act.activation(k_t[:], w1[:], ACT.Identity, bias=bk_c[:]).then_inc(k_sb, 1)

            def logits(R, tile):
                act.wait_ge(lg_ps, R + 1)
                act.copy(lg_all[:, bass.ds(tile, TB), :], ps_lg).then_inc(lg_sb, 1)

            def scores(a):
                act.wait_ge(s_ps, a + 1)
                act.wait_ge(nm_done, a + 1)
                act.copy(sc[:], w0[:]).then_inc(sc_sb, 1)

            def norm_r(A):
                act.wait_ge(nw2, A * (N_NW + 1) + (N_NW + 1))
                act.wait_ge(x2_done, A + 1)
                for k in range(TB):
                    act.activation(rn[:, k, :], rr[:, k, :], ACT.Identity,
                                   bias=nmr[:, k:k + 1], scale=rstd[:, AFTER_AT + k:AFTER_AT + k + 1]).then_inc(rn_done, 1)

            def shared(R):
                act.wait_ge(shG, R + 1)
                act.wait_ge(shh, R + 1)
                act.activation(sg[:], w0[:].rearrange("p t d -> p (t d)"), ACT.Silu).then_inc(sg_done, 1)

            def exps(a):
                act.wait_ge(nm_done, a + 2)
                act.wait_ge(pr_done, (a + 1) * TB)
                for k in range(TB):
                    act.activation(ex[:, k, :], sc[:, k, :], ACT.Exp, bias=nmax[:, k:k + 1], scale=SCALE).then_inc(ex_done, 1)

            def gates_of_layer(n, first, hs):
                for k, count in ((0, 1), (1, 7)):
                    slots(first, hs[2 * k:2 * k + 2])
                    act.wait_ge(tl, n * 9 + count)
                    t, s = ((gt[:], gt[:]), (g4[:, 4, :], g4[:, 3, :]))[k]
                    act.activation(t, s, ACT.Exp).then_inc(tl_e, 1)
                slots(first, hs[4:])

            def turn_block(B, k):
                act.wait_ge(xT_ps, B + 5)
                act.wait_ge(u_ps, B + 1)
                act.activation(x_t[:, k, :], ps_x[:, 0, :], ACT.Identity, bias=bf_c[:], scale=gf_c[:]).then_inc(xT_sb, 1)

            def slot(B, k4, half, x=True, up=True, down=True, turn=True):
                k = k4 % 2
                if half == 0 and up:
                    act.wait_ge(g_ps, B + 1)
                    act.wait_ge(h_done, B + 1)
                    act.activation(sil[:, k, :], ff(ps_g), ACT.Silu).then_inc(sil_done, 1)
                if half == 1 and x:
                    turn_block(B + 1, 1 - k)
                if half == 1 and down:
                    r4 = (k4 - 2) % 4
                    act.wait_ge(y_ps, B + 1)
                    act.wait_ge(yst[r4], (B - (2 + r4)) * 4 + 16)
                    act.copy(yb[:, r4, :], ps_y[:, 0, :]).then_inc(y_sb, 1)
                if half == 1 and turn:
                    act.wait_ge(hT_ps, B + 2)
                    act.wait_ge(y_ps, B)
                    act.copy(h_t[:, 1 - k, :], ff(ps_h)).then_inc(hT_sb, 1)

            def slots(first, hs):
                for b, half in hs:
                    slot(first + b, b % 4, half, x=b + 1 < NBLK, up=b < NBLK, down=b >= 2, turn=1 <= b <= NBLK)

            def loop(B):
                for b, half in LOOP:
                    slot(B + b, b % 4, half)

            def output(C, tile):
                act.wait_ge(cb, C * N_CB + 3 * N_CB)
                act.dma_start(out[bass.ds(tile, TB)].rearrange("t p d -> p t d"), xres[:, bass.ds(tile, TB), :]).then_inc(out_st, 16)

            def route(R, parts):
                slots(0, parts[0])
                turn_z(R)
                logits(R, R * TB)
                slots(0, parts[2])
                shared(R)
                slots(0, parts[4] + parts[5])

            turn_z(0)
            logits(0, 0)
            for R in range(BPG):
                shared(R)
                if R + 1 < BPG:
                    turn_z(R + 1)
                expert(2 * R)
                if R + 1 < BPG:
                    logits(R + 1, (R + 1) * TB)
                expert(2 * R + 1)
            route(BPG, ALONE)
            turn_block(0, 0)
            for n in range(1, BPG):
                route(BPG + n, share(ROUTED, n - 1))
            with act.Fori(AFTER_ROUTED, NBLK // 8 - 1) as i:
                loop(i * 8)
            gates_of_layer(0, 0, LAST8)
            turn_block(NBLK, 0)
            slots(0, DRAIN)
            with act.Fori(0, NG) as g:
                first = g * NBLK + NBLK
                before = share(SHARES, 0)
                slots(first, before[0])
                turn_x(g * BPG)
                slots(first, before[1])
                queries(g * BPG)
                keys(g * BPG)
                slots(first, before[2])
                for s in range(STEPS):
                    parts, (a, A, R), p = share(SHARES, s + 1), stages(s), ahead(s)
                    tile = g * TPG + s * TB
                    a, A, p = (None if n is None else g * BPG + n for n in (a, A, p))
                    R = None if R is None else g * BPG + (R2 + R)
                    if a is not None:
                        scores(a)
                    if A is not None:
                        turn_p(A)
                    slots(first, parts[0])
                    if A is not None:
                        mix(A)
                    slots(first, parts[1])
                    if R is not None:
                        turn_z(R)
                    if p is not None:
                        turn_x(p)
                    slots(first, parts[2])
                    if R is not None:
                        logits(R, tile + (-2 * TB))
                    if p is not None:
                        queries(p)
                        keys(p)
                    slots(first, parts[3])
                    if a is None and A is not None:
                        norm_r(A)
                    if R is not None:
                        shared(R)
                    if a is not None:
                        exps(a)
                    slots(first, parts[4])
                    if a is not None and A is not None:
                        norm_r(A)
                    slots(first, parts[5])
                slots(first, DRAIN)
                turn_block(first + NBLK, 0)
            gates_of_layer(1, 3 * NBLK, FIRST)
            with act.Fori(0, BPG) as i:
                loop(i * 8 + (3 * NBLK + 4))
                output(i + R2, i * TB)
            slots(3 * NBLK, LAST)
            with act.Fori(0, BPG) as i:
                output(i + (R2 + BPG), i * TB + TPG)

        @block.vector
        def _(dve):
            dve.memset(pads[:, :, 0:D], 0.0).then_inc(pad_z, 1)
            def expert(e):
                dve.wait_ge(wt_ps, 2 + e)
                dve.tensor_copy(gu_t[:, e, FF:2 * FF], ff((ps_u, ps_y)[e % 2])).then_inc(wt_v, 1)

            def row(t):
                return t.rearrange("p t d -> p (t d)")

            def res(tile, k):
                return row(xres[:, bass.ds(tile + k, 1), :])

            def links(chain, at):
                n = [0]

                def link(ins, by=1):
                    n[0] += by
                    ins.then_inc(chain, by)
                    dve.wait_ge(chain, at + n[0])
                return link, n

            def stats(src, lo, bn, ag, at):
                for k in range(TB):
                    dve.bn_stats(bn6[:, lo + k, :], src(k)).then_inc(bn, 1)
                for k in range(TB):
                    dve.wait_ge(bn, at + (k + 1))
                    apart(dve)
                    dve.bn_aggr(mv[:, lo + k, :], bn6[:, lo + k, :]).then_inc(ag, 1)

            def stats_before(a, tile):
                dve.wait_ge(cb, a * N_CB + 3 * N_CB)
                apart(dve)
                stats(lambda k: res(tile, k), 0, bn1, ag1, a * TB)

            def stats_after(A):
                dve.wait_ge(rr_done, A * TB + TB)
                apart(dve)
                stats(lambda k: rr[:, k, :], AFTER_AT, bn2, ag2, A * TB)

            def stats_route(R, A, tile):
                dve.wait_ge(x2_done, A + 2)
                apart(dve)
                stats(lambda k: res(tile, k), ROUTE_AT, bn3, ag3, R * TB)

            N_NORM = 2 + 3 * NSTEP

            def newton(n, chain, at, lo, mid, hi):
                w, y, t = (b[:, lo:hi] for b in (var_e, rstd, nw_t))
                by = 1
                if n:
                    dve.wait_ge(chain, at + (n + 1))
                if n == 0:
                    if lo < mid:
                        u = dve.tensor_scalar(var_e[:, lo:mid], mv[:, lo:mid, 1], 1.0, EPS, ALU.mult, ALU.add)
                        u.then_inc(chain, 1 if hi > mid else 2)
                    if hi > mid:
                        u = dve.tensor_scalar(var_e[:, mid:hi], mv[:, mid:hi, 1], 1.0 + EPS, EPS * EPS, ALU.mult, ALU.add)
                        u.then_inc(chain, 1 if lo < mid else 2)
                    return
                if n == 1:
                    u = dve.tensor_scalar(y.bitcast(I32), w.bitcast(I32), -0.5, RSQRT_SEED, ALU.mult, ALU.add)
                elif n % 3 == 2:
                    u = dve.scalar_tensor_tensor(t, y, -0.5, y, ALU.mult, ALU.mult)
                elif n % 3 == 0:
                    u = dve.tensor_tensor(t, t, w, ALU.mult)
                else:
                    u = dve.scalar_tensor_tensor(y, t, 1.5, y, ALU.add, ALU.mult)
                u.then_inc(chain, 1)
                if n == N_NORM - 1:
                    dve.wait_ge(chain, at + N_NW)

            def norms_after(n, A):
                if n == 0:
                    dve.wait_ge(ag2, A * TB + TB)
                if n < N_NORM:
                    newton(n, nw2, A * (N_NW + 1), AFTER_AT, AFTER_AT + TB, AFTER_AT + TB)
                else:
                    dve.scalar_tensor_tensor(nmr[:], mv[:, AFTER_AT:AFTER_AT + TB, 0], -1.0, rstd[:, AFTER_AT:AFTER_AT + TB],
                                             ALU.mult, ALU.mult).then_inc(nw2, 1)

            def first_stats(R):
                if R <= BPG:
                    dve.wait_ge(ld_x[R], 16)
                stats(lambda k: res(R * TB, k), R * TB, bn3, ag3, R * TB)

            def first_norms(J, lo, hi):
                dve.wait_ge(ag3, hi)
                for m in range(N_NORM):
                    newton(m, nw, J * N_NW, lo, lo, hi)

            def norm_x(n, tile):
                for k in range(TB):
                    dve.tensor_scalar(xn[n][:, k, :], res(tile, k), mv[:, k, 0:1], rstd[:, k:k + 1],
                                      ALU.subtract, ALU.mult).then_inc(xn_done, 1)

            def norm_z(R, n, tile, col, used=True):
                if used:
                    dve.wait_ge(scat[n], (R - n) * (N_SCAT // BPG))
                for k in range(TB):
                    src = xres[:, bass.ds(tile + k, 1), :].broadcast_to([P, 2, D])
                    dve.tensor_scalar(zz[n][:, k, :, 0:D], src, mv[:, col + k, 0:1], rstd[:, col + k:col + k + 1],
                                      ALU.subtract, ALU.mult).then_inc(z_done, 1)

            def bc(t):
                return t.rearrange("p (t o) -> p t o", o=1).broadcast_to([P, TB, NE])

            def tokens(t):
                return t.rearrange("p (o e) -> p o e", o=1).broadcast_to([P, TB, NE])

            def pick(n, R, tile):
                fw = tokens(first_w[:])
                lg = lg_all[:, bass.ds(tile, TB), :]
                m1 = m1_all[:, bass.ds(tile, TB)]
                oh1 = oh_all[0][:, bass.ds(tile, TB), :]
                oh2 = oh_all[1][:, bass.ds(tile, TB), :]
                if n:
                    dve.wait_ge(rc, R * N_RC + n)
                else:
                    dve.wait_ge(lg_sb, R + 1)
                if n == 0:
                    t = dve.tensor_reduce(m1, lg, AX_X, ALU.max)
                elif n == 1:
                    t = dve.tensor_tensor(r8[:], lg, bc(m1), ALU.is_equal)
                elif n == 2 or n == 8:
                    t = dve.tensor_tensor(r8[:], r8[:], fw, ALU.mult)
                elif n == 3 or n == 9:
                    t = dve.tensor_reduce(f4[:], r8[:], AX_X, ALU.max)
                elif n == 4:
                    t = dve.tensor_tensor(oh1, fw, bc(f4[:]), ALU.is_equal)
                elif n == 5:
                    t = dve.scalar_tensor_tensor(r8b[:], oh1, TAKEN, lg, ALU.mult, ALU.add)
                elif n == 6:
                    t = dve.tensor_reduce(f4[:], r8b[:], AX_X, ALU.max)
                elif n == 7:
                    t = dve.tensor_tensor(r8[:], r8b[:], bc(f4[:]), ALU.is_equal)
                elif n == 10:
                    t = dve.tensor_tensor(oh2, fw, bc(f4[:]), ALU.is_equal)
                if n < N_PICK:
                    t.then_inc(rc, 1)
                else:
                    dve.tensor_tensor(sel[:, TB:2 * TB, :], oh1, oh2, ALU.add).then_inc(sel_done, 1)

            def shared(R):
                dve.wait_ge(shU, R + 1)
                dve.wait_ge(sg_done, R + 1)
                dve.tensor_tensor(sh[:].rearrange("p t d -> p (t d)"), sg[:], w1[:].rearrange("p t d -> p (t d)"),
                                  ALU.mult).then_inc(shh, 1)

            def rows(m, R, s, tile):
                oh1 = oh_all[0][:, bass.ds(tile, TB), :]
                oh2 = oh_all[1][:, bass.ds(tile, TB), :]
                if m == 0:
                    dve.wait_ge(pf_ps, R + 1)
                dve.wait_ge(rc, R * N_RC + (N_PICK + m))
                if m == 0:
                    t = dve.tensor_tensor(pos[:], ps_pf[:, 0:TB, :], tokens(run[:]), ALU.add)
                elif m == 1:
                    t = dve.tensor_tensor(run[:], run[:], ps_pf[:, TB, :], ALU.add)
                elif m == 2:
                    t = dve.tensor_tensor(r8[:], oh1, pos[:], ALU.mult)
                elif m == 3:
                    t = dve.tensor_tensor(r8b[:], oh2, pos[:], ALU.mult)
                elif m == 4:
                    t = dve.tensor_reduce(s[:, 0, :], r8[:], AX_X, ALU.add)
                elif m == 5:
                    t = dve.tensor_reduce(s[:, 1, :], r8b[:], AX_X, ALU.add)
                t.then_inc(rc, 1)

            def shared_joins(R, tile):
                dve.wait_ge(shD, R + 1)
                xr = xres[:, bass.ds(tile, TB), :]
                dve.scalar_tensor_tensor(xr, w0[:], 0.5, xr, ALU.mult, ALU.add).then_inc(xr_done, 1)

            def gates_of_layer(l, first, bs):
                link, n = links(tl, l * 9)
                m1 = m1_all[:].rearrange("p (t o) -> p t o", o=1).broadcast_to([P, NT, NE])
                link(dve.tensor_tensor(gt[:], lg_all[:], m1, ALU.subtract))
                slot(first + bs[0], bs[0] % 4)
                dve.wait_ge(tl_e, l * 2 + 1)
                link(dve.tensor_reduce(g4[:, 0, :], gt[:], AX_X, ALU.add))
                link(dve.tensor_tensor(gt[:], gt[:], oh_all[1][:], ALU.mult))
                link(dve.tensor_reduce(g4[:, 1, :], gt[:], AX_X, ALU.add))
                link(dve.reciprocal(g4[:, 2, :], g4[:, 0, :]))
                link(dve.tensor_scalar(g4[:, 1, :], g4[:, 1, :], 1.0, None, ALU.subtract))
                link(dve.tensor_tensor(g4[:, 3, :], g4[:, 1, :], g4[:, 2, :], ALU.mult))
                slot(first + bs[1], bs[1] % 4)
                dve.wait_ge(tl_e, l * 2 + 2)
                link(dve.tensor_scalar(g4[:, 5, :], g4[:, 4, :], 2.0, 2.0, ALU.mult, ALU.add))
                link(dve.reciprocal(gates[:, 0, :], g4[:, 5, :]))
                assert n[0] == 9
                dve.tensor_tensor(gates[:, 1, :], gates[:, 0, :], g4[:, 4, :], ALU.mult).then_inc(gts, 1)
                for b in bs[2:]:
                    slot(first + b, b % 4)

            def region(g):
                return row(region0[:, bass.ds(g, 1), :])

            def region_ends(ph):
                dve.tensor_copy(ends[:, bass.ds(ph * NE, NE)], run[:]).then_inc(ended, 1)

            def block_list(ph, g, between=lambda: None):
                N = 12
                link, n = links(bl, ph * N)
                bn = blk_no[:].rearrange("p (b o) -> p b o", o=1).broadcast_to([P, NBLK, NE])

                def every(t):
                    return t.rearrange("p (o e) -> p o e", o=1).broadcast_to([P, NBLK, NE])
                link(dve.tensor_tensor(cnt[:], run[:], region(g), ALU.subtract))
                link(dve.tensor_tensor(cmp16[:], cnt[:].rearrange("p (e o) -> p e o", o=1).broadcast_to([P, NE, TPG]),
                                       full_at[:].rearrange("p (o t) -> p o t", o=1).broadcast_to([P, NE, TPG]), ALU.is_gt))
                link(dve.tensor_reduce(nbk[:], cmp16[:], AX_X, ALU.add))
                between()
                apart(dve)
                link(dve.tensor_tensor_scan(bend[:], one_f[:, 0:NE], nbk[:], 0.0, ALU.mult, ALU.add))
                link(dve.tensor_tensor(cmpb[:], bn, every(bend[:]), ALU.is_ge))
                link(dve.tensor_reduce(be[:], cmpb[:], AX_X, ALU.add))
                between()
                link(dve.tensor_tensor(cmpb2[:], cmpb[:], every(nbk[:]), ALU.mult))
                link(dve.tensor_reduce(bs[:], cmpb2[:], AX_X, ALU.add))
                link(dve.tensor_tensor(bt[:], blk_no[:], bs[:], ALU.subtract))
                base = row(region0[:, bass.ds(g, 1), 0:1]).broadcast_to([P, NBLK])
                link(dve.scalar_tensor_tensor(bt[:], bt[:], float(P), base, ALU.mult, ALU.add))
                at = bass.ds(ph * NBLK, NBLK)
                link(dve.scalar_tensor_tensor(tab_r[:, at], be[:], float(REGION), bt[:], ALU.mult, ALU.add))
                between()
                link(dve.tensor_scalar(be[:], be[:], float(NE - 1), None, ALU.min))
                assert n[0] == N
                dve.tensor_scalar(tab_w[:, at], be[:], float(FF), None, ALU.mult).then_inc(tab, 1)

            def start_group(ph, g):
                dve.tensor_copy(run[:], region(g)).then_inc(run0, 1)
                dve.wait_ge(run0, ph + 1)

            def combine(C, n, tile):
                dve.wait_ge(yld[n], (C - n) * 8 + 16)
                join(C, yg[n], tile)

            def join(C, y, tile):
                for c in range(2):
                    for k in range(TB):
                        if c:
                            dve.wait_ge(cb, C * N_CB + (2 * N_CB + k + 1))
                        dve.scalar_tensor_tensor(res(tile, k), y[:, k, c, :], gates[:, c, bass.ds(tile + k, 1)],
                                                 res(tile, k), ALU.mult, ALU.add).then_inc(cb, 1)

            def leaky(A, n):
                dve.wait_ge(o_sb, A + 2)
                dve.scalar_tensor_tensor(lr[:], o[:], SLOPE, o[:], ALU.mult, ALU.max).then_inc(lr_done, 1)
                dve.wait_ge(lr_done, A + 2)
                dve.wait_ge(rn_done, A * TB + TB)
                for k in range(TB):
                    dve.scalar_tensor_tensor(rr[:, k, :], lr[:, k, :], rinv[:, k:k + 1], xn[n][:, k, :],
                                             ALU.mult, ALU.add).then_inc(rr_done, 1)

            def values(a):
                dve.wait_ge(v_ps, a + 1)
                dve.wait_ge(o_ps, a + 1)
                dve.tensor_tensor(v[:], w1[:], bv_b[:].rearrange("p (o d) -> p o d", o=1).broadcast_to([P, TB, D]),
                                  ALU.add).then_inc(v_sb, 1)

            def search(a, between):
                n = 0
                dve.wait_ge(sc_sb, a + 1)
                apart(dve)
                for r in range(KTOP // 8):
                    at = a * N_TOP + 2 * TB * r
                    src = wk_s if r else sc
                    eight = slice(8 * r, 8 * r + 8)
                    for k in range(TB):
                        if r:
                            dve.wait_ge(tk, at + (k + 1 - TB))
                            apart(dve)
                        dve.max(top[:, k, eight], src[:, k, :]).then_inc(tk, 1)
                        between(n)
                        n += 1
                    for k in range(TB):
                        dve.wait_ge(tk, at + (k + 1))
                        apart(dve)
                        dve.match_replace(wk_s[:, k, :], top[:, k, eight], src[:, k, :], TAKEN).then_inc(tk, 1)
                        between(n)
                        n += 1
                    if r == 0:
                        dve.tensor_scalar(nmax[:], top[:, :, 0], -SCALE, None, ALU.mult).then_inc(nm_done, 1)

            def probabilities(a):
                for k in range(TB):
                    dve.wait_ge(tk, a * N_TOP + (N_TOP - TB + k + 1))
                    dve.wait_ge(ex_done, a * TB + (k + 1))
                    dve.scalar_tensor_tensor(pr[:, k, :], wk_s[:, k, :], TAKEN_BELOW, ex[:, k, :], ALU.is_lt, ALU.mult,
                                             accum_out=psum_p[:, k:k + 1]).then_inc(pr_done, 1)
                dve.wait_ge(pr_done, a * TB + 2 * TB)
                dve.reciprocal(rinv[:], psum_p[:]).then_inc(ri_done, 1)
                dve.wait_ge(ri_done, a + 1)

            def slot(B, k4):
                k = k4 % 2
                dve.wait_ge(u_ps, B + 3)
                dve.wait_ge(sil_done, B + 3)
                dve.wait_ge(hT_ps, B + 1)
                dve.tensor_tensor(h[:, k, :], sil[:, k, :], ff(ps_u), ALU.mult).then_inc(h_done, 1)

            def slots(first, hs):
                for b, half in hs:
                    if half == 0 and b < NBLK:
                        slot(first + b, b % 4)

            def route(R, parts):
                n, tile = R - BPG, R * TB
                slots(0, parts[0])
                if n + 1 < BPG:
                    norm_z(R + 1, n + 1, tile + TB, tile + TB)
                for m in range(N_PICK + 1):
                    pick(m, R, tile)
                slots(0, parts[2])
                shared(R)
                slots(0, parts[4])
                for m in range(N_ROWS):
                    rows(m, R, s_idx[n], tile)
                shared_joins(R, tile)
                more = [p for p in parts[5] if p[1] == 0]
                if n == BPG - 1:
                    region_ends(1)
                    block_list(1, 1, lambda: slots(0, [more.pop(0)] if more else []))
                slots(0, more)

            first_stats(0)
            first_norms(0, 0, TB)
            norm_z(0, 0, 0, 0, used=False)
            dve.wait_ge(wt_ps, 1)
            dve.tensor_copy(sm_t[:, 3:6, :], w1[:, 0:3, :])
            dve.tensor_copy(rw_t[:], ps_lg[:, 0, :]).then_inc(wt_v, 1)
            for R in range(1, BPG):
                first_stats(R)
            dve.wait_ge(cst, 1)
            start_group(0, 0)
            for R in range(BPG):
                tile = R * TB
                for m in range(N_PICK + 1):
                    pick(m, R, tile)
                if R:
                    shared_joins(R - 1, tile - TB)
                    expert(2 * R - 1)
                for m in range(N_ROWS):
                    rows(m, R, s_idx[R], tile)
                shared(R)
                if R == 0:
                    first_norms(1, TB, TPG)
                    for n in range(1, BPG):
                        norm_z(n, n, n * TB, n * TB, used=False)
                if R == BPG - 1:
                    region_ends(0)
                first_stats(BPG + R)
                if R == BPG - 1:
                    first_norms(2, TPG, NT)
                    norm_z(BPG, 0, TPG, TPG)
                expert(2 * R)
            shared_joins(BPG - 1, TPG - TB)
            expert(2 * BPG - 1)
            block_list(0, 0)
            start_group(1, 1)
            for n in range(BPG):
                route(BPG + n, share(ROUTED, n - 1) if n else ALONE)
            dve.wait_ge(ld_c, 16 * 7)
            with dve.Fori(AFTER_ROUTED, NBLK // 8 - 1) as i:
                for q in range(8):
                    slot(i * 8 + q, q % 4)
            gates_of_layer(0, 0, range(NBLK - 8, NBLK))
            with dve.Fori(0, NG) as g:
                ph, first = g + 2, g * NBLK + NBLK
                dve.wait_ge(gts, 1)
                start_group(ph, g)
                def norms(n, J, p, R):
                    if n == 0:
                        for b, ag in ((p, ag1), (R, ag3)):
                            if b is not None:
                                dve.wait_ge(ag, b * TB + TB)
                    newton(n, nw, J * N_NW, 0 if p is not None else ROUTE_AT, ROUTE_AT, ROUTE_AT + TB if R is not None else ROUTE_AT)

                J0 = g * (1 + STEPS) + FIRST_NORMS
                ups = [[q for q in part if q[1] == 0] for part in share(SHARES, 0)]
                slots(first, ups[0][:3])
                combine(g * BPG, 0, g * TPG)
                stats_before(g * BPG, g * TPG)
                for m in range(N_NORM):
                    norms(m, J0, g * BPG, None)
                    if m in (4, 8):
                        slots(first, ups[0][3 + m // 8:4 + m // 8])
                norm_x(0, g * TPG)
                slots(first, ups[0][5:])
                combine(g * BPG + 1, 1, g * TPG + TB)
                stats_before(g * BPG + 1, g * TPG + TB)
                slots(first, ups[1] + ups[2])
                for s in range(STEPS):
                    parts, (a, An, Rg), pn = share(SHARES, s + 1), stages(s), ahead(s)
                    J, tile = J0 + (s + 1), g * TPG + s * TB
                    a, A, B, p = (None if m is None else g * BPG + m for m in (a, An, Rg, pn))
                    R = None if Rg is None else g * BPG + (R2 + Rg)
                    rt = tile + (-2 * TB)
                    ups = [[q for q in part if q[1] == 0] for part in parts]
                    hooks = {}
                    for at, part in zip(HOOKS if a is not None else HOOKS_LATE if A is not None else HOOKS_LAST, ups):
                        assert len(part) <= len(at)
                        hooks.update(zip(at, part))
                    after = AFTER if a is not None else AFTER_LATE
                    if R is not None:
                        stats_route(R, B, rt)

                    def between(m):
                        if m < N_NORM and (p is not None or R is not None):
                            norms(m, J, p, R)
                        if m == VALUES and a is not None:
                            values(a)
                        if m == ROUTE_ROWS and R is not None:
                            norm_z(R, Rg, rt, ROUTE_AT)
                        if m == NEXT_ROWS and p is not None:
                            norm_x(pn, tile + TB)
                        if m == after and A is not None:
                            leaky(A, An)
                        if m == after + 1 and A is not None:
                            stats_after(A)
                        if after + 2 <= m <= after + 2 + N_NORM and A is not None:
                            norms_after(m - (after + 2), A)
                        if PICKS <= m <= PICKS + N_PICK and R is not None:
                            pick(m - PICKS, R, rt)
                        if m == (SHARED if a is not None else SHARED_LATE) and R is not None:
                            shared(R)
                        if m in hooks:
                            slots(first, (hooks[m],))
                    if a is not None:
                        search(a, between)
                        probabilities(a)
                    else:
                        for m in range(N_TOP):
                            between(m)
                    more = list(ups[5])
                    if R is not None:
                        shared_joins(R, rt)
                        for m in range(N_ROWS):
                            rows(m, R, s_idx[Rg], rt)
                            if m % 3 == 1 and more:
                                slots(first, [more.pop(0)])
                    if s == STEPS - 1:
                        region_ends(ph)
                        block_list(ph, g, lambda: slots(first, [more.pop(0)] if more else []))
                    slots(first, more)
                    if s + 2 < BPG:
                        combine(a + 2, s % 2, tile + 2 * TB)
                        stats_before(a + 2, tile + 2 * TB)
            gates_of_layer(1, 3 * NBLK, range(4))
            dve.wait_ge(gts, 2)
            with dve.Fori(0, BPG // 2) as i:
                for n in range(2):
                    for q in range(8):
                        slot(i * 16 + (3 * NBLK + 8 * n + 4 + q), q % 4)
                    combine(i * 2 + (R2 + n), n, i * (2 * TB) + n * TB)
            for b in range(NBLK - 4, NBLK):
                slot(3 * NBLK + b, b % 4)
            for n in range(BPG):
                dve.wait_ge(yld_last[n], 16)
                join(R2 + BPG + n, yg_last[n], TPG + n * TB)

        @block.gpsimd
        def _(pool):
            pool.memset(sel[:], 0.0).then_inc(pc, 1)
            pool.memset(one_f[:], 1.0).then_inc(pc, 1)
            pool.memset(ones[:], 1.0).then_inc(pc, 1)
            pool.wait_ge(pc, 3)
            pool.affine_select(out=ident[:], in_=one_f[:], compare_op=ALU.is_equal, fill=0.0, base=0,
                               pattern=[[-1, P]], channel_multiplier=1)
            pool.affine_select(out=upper[:], in_=ones[:], compare_op=ALU.is_ge, fill=0.0, base=-1,
                               pattern=[[1, P]], channel_multiplier=-1)

            def count(t, pattern, base=0, rows=0):
                return pool.iota(t, pattern=pattern, base=base, channel_multiplier=rows, allow_small_or_imprecise_dtypes=True)
            count(first_w[:], [[-1, NE]], NE)
            count(region0[:], [[GROUP_ROWS, NG], [REGION, NE]])
            count(full_at[:], [[P, TPG]])
            count(blk_no[:], [[1, NBLK]])
            count(result_no[:], [[2 * P, NT], [1, 2]], 0, 2)
            count(pads[:, :, D].bitcast(I32), [[P, NE + SPARE]], RESULTS, 1).then_inc(pc, 1)
            pool.wait_ge(pc, 4)
            pool.nop().then_inc(cst, 1)
            pool.wait_ge(pad_z, 1)
            for k in range(4):
                g, s = k // 2, k % 2 * (SPARE // 2)
                r = g * GROUP_ROWS + NE * REGION + s * P
                pool.dma_start(xs[r:r + SPARE // 2 * P].rearrange("(s p) d -> p s d", p=P),
                               pads[:, NE + s:NE + s + SPARE // 2, :]).then_inc(yst[k], 16)
            pool.wait_ge(ld_c, 16 * 7)

            def wide(t):
                return t[:].rearrange("p (o d) -> p o d", o=1).broadcast_to([P, TB, D])

            def number(R, n, tile):
                pool.wait_ge(rc, R * N_RC + N_RC)
                apart(pool)
                pool.tensor_copy(zz[n][:, :, :, D].bitcast(I32), result_no[:, bass.ds(tile, TB), :]).then_inc(ids, 1)
                pool.wait_ge(ids, R + 1)
                apart(pool)

            def scatter(n, ks):
                for k in ks:
                    for c in range(2):
                        pool.indirect_dma_start(xs, bass.IndirectOffsetOnAxis(s_idx[n][:, c, k:k + 1], 0),
                                                zz[n][:, k, c, :], None).then_inc(scat[n], 16)

            def attended(A, tile):
                pool.wait_ge(rn_done, A * TB + 2 * TB)
                pool.tensor_tensor(rg[:], rn[:], wide(ga_b), ALU.mult).then_inc(rg_done, 1)
                pool.wait_ge(rg_done, A * 2 + 1)
                pool.tensor_tensor(rg[:], rg[:], wide(ba_b), ALU.add).then_inc(rg_done, 1)
                pool.wait_ge(rg_done, A * 2 + 2)
                xr = xres[:, bass.ds(tile, TB), :]
                pool.tensor_tensor(xr, xr, rg[:], ALU.add).then_inc(x2_done, 1)

            def slot(B, k4, copy=True, store=True):
                if copy:
                    pool.wait_ge(xT_ps, B + 5)
                    pool.wait_ge(yst[k4], (B - k4) * 4 + 16)
                    apart(pool)
                    pool.tensor_copy(idx[:, k4:k4 + 1], xin[:, k4, D:D + 1].bitcast(I32)).then_inc(idx_cp, 1)
                if store:
                    r4 = (k4 - 2) % 4
                    pool.wait_ge(y_sb, B + 1)
                    pool.wait_ge(idx_cp, B + 3)
                    apart(pool)
                    pool.indirect_dma_start(yt, bass.IndirectOffsetOnAxis(idx[:, r4:r4 + 1], 0),
                                            yb[:, r4, :], None).then_inc(yst[r4], 16)

            def slots(first, hs):
                for b, half in hs:
                    if half == 1:
                        slot(first + b, b % 4, copy=b < NBLK, store=b >= 2)

            for R in range(BPG):
                number(R, R, R * TB)
                scatter(R, range(TB))
            for n in range(BPG):
                parts = share(ROUTED, n - 1) if n else ALONE
                for part in parts[:5]:
                    slots(0, part)
                number(BPG + n, n, TPG + n * TB)
                scatter(n, range(TB // 2))
                slots(0, parts[5][:2])
                scatter(n, range(TB // 2, TB))
                slots(0, parts[5][2:])
            with pool.Fori(AFTER_ROUTED, NBLK // 8 - 1) as i:
                for q in range(8):
                    slot(i * 8 + q, q % 4)
            slots(0, LAST8 + DRAIN)
            with pool.Fori(0, NG) as g:
                first = g * NBLK + NBLK
                for part in share(SHARES, 0):
                    slots(first, part)
                for s in range(STEPS):
                    parts, (a, A, R) = share(SHARES, s + 1), stages(s)
                    n, tile = R, g * TPG + s * TB
                    A = None if A is None else g * BPG + A
                    R = None if R is None else g * BPG + (R2 + R)
                    until = 5 if a is not None else 4
                    for part in parts[:until]:
                        slots(first, part)
                    if A is not None:
                        attended(A, tile + (-TB))
                    for part in parts[until:5]:
                        slots(first, part)
                    if R is None or a is None:
                        late = parts[5]
                    else:
                        slots(first, parts[5])
                        late = []
                    if R is not None:
                        number(R, n, tile + (-2 * TB))
                        scatter(n, range(TB // 2))
                    slots(first, late[:2])
                    if R is not None:
                        scatter(n, range(TB // 2, TB))
                    slots(first, late[2:])
                slots(first, DRAIN)
            slots(3 * NBLK, FIRST)
            with pool.Fori(0, NBLK // 8 - 1) as i:
                for q in range(8):
                    slot(i * 8 + (3 * NBLK + 4 + q), q % 4)
            slots(3 * NBLK, LAST)


def kernel(L0_attn_x, L0_attn_Wq, L0_attn_bq, L0_attn_Wk, L0_attn_bk, L0_attn_Wv, L0_attn_bv, L0_attn_gamma,
           L0_attn_beta, L0_ffn_ln_gamma, L0_ffn_ln_beta, L0_ffn_router_w, L0_ffn_gate_up_w, L0_ffn_down_w,
           L0_ffn_shared_gate_up_w, L0_ffn_shared_down_w):
    import numpy as np
    import concourse.bacc as bacc
    from concourse.bass_utils import run_bass_kernel_spmd

    nc = bacc.Bacc("TRN2", target_bir_lowering=False, num_devices=1)
    given = dict(x=np.ascontiguousarray(L0_attn_x).reshape(NT, P, D), wq=L0_attn_Wq, bq=L0_attn_bq, wk=L0_attn_Wk,
                 bk=L0_attn_bk, wv=L0_attn_Wv, bv=L0_attn_bv, ga=L0_attn_gamma, ba=L0_attn_beta, gf=L0_ffn_ln_gamma,
                 bf=L0_ffn_ln_beta, rw=L0_ffn_router_w, guw=L0_ffn_gate_up_w, dnw=L0_ffn_down_w,
                 sguw=L0_ffn_shared_gate_up_w, sdnw=L0_ffn_shared_down_w)
    arrays = {f"in_{n}": np.ascontiguousarray(a) for n, a in given.items()}
    args = [nc.dram_tensor(n, a.shape, mybir.dt.from_np(a.dtype), kind="ExternalInput").ap() for n, a in arrays.items()]
    out = nc.dram_tensor("out", (NT, P, D), F32, kind="ExternalOutput").ap()
    xs = nc.dram_tensor("rows", (NG * GROUP_ROWS, XW), F32).ap()
    yt = nc.dram_tensor("results", (RESULTS + (NE + SPARE) * P, D), F32).ap()
    macaron(nc, *args, out, xs, yt)
    r = run_bass_kernel_spmd(nc, [arrays], core_ids=[0])
    return r.results[0]["out"].reshape(L0_attn_x.shape)
```
